# Optimizing a Trainium2 kernel written in Bass

```python
import numpy as np
import jax
import jax.numpy as jnp

def _softmax(x, axis=-1):
    return jax.nn.softmax(x, axis=axis)
def _gelu(x):
    return jax.nn.gelu(x, approximate=True)
def _silu(x):
    return jax.nn.silu(x)
def _sigmoid(x):
    return jax.nn.sigmoid(x)
def _layernorm(x, axis=-1, eps=1e-5):
    m = jnp.mean(x, axis=axis, keepdims=True)
    v = jnp.var(x, axis=axis, keepdims=True)
    return (x - m) / jnp.sqrt(v + eps)
def _scatter_add(tgt, idx, src, axis=0):
    return tgt.at[idx].add(src)
def _segment_sum(src, seg, n):
    return jax.ops.segment_sum(src, seg, n)

kernel_name = 'mk_vit_tower_d1_tok_img256_7a7a50'

def setup_inputs(seed: int = 0):
    np.random.seed(seed)
    _w = jnp.asarray
    def _rec_inputs():
        import jax
        import jax.numpy as jnp
        _rk = jax.random.key(seed)
        x = (-0.00016672 + 0.999947 * jax.random.normal(jax.random.fold_in(_rk, 1), (32, 3, 336, 336), jnp.float32))
        return x
    x = _rec_inputs()
    def _L0_tok_setup():
        import jax, jax.numpy as jnp
        import numpy as np
        PATCH = 16
        key = jax.random.key(seed)
        k1, k2, k3 = jax.random.split(key, 3)
        B, C, H, Wd = (64, 3, 384, 384)
        E = 256
        pdim = PATCH * PATCH * C
        x = jax.random.normal(k1, (B, C, H, Wd), dtype=jnp.float32)
        W = jax.random.normal(k2, (E, pdim), dtype=jnp.float32) * pdim ** (-0.5)
        b = jax.random.normal(k3, (E,), dtype=jnp.float32) * 0.01
        return {'x': x, 'W': W, 'b': b}
    _L0_tok_all = _L0_tok_setup()
    _L0_tok_in = {k: v for k, v in _L0_tok_all.items() if k in ('W', 'b', )}
    del _L0_tok_all

    def _L0_attn_setup():
        import jax, jax.numpy as jnp
        import numpy as np
        HEADS = 8
        DIM_HEAD = 64
        KNN = 32
        SCALE = DIM_HEAD ** (-0.5)

        def _knn_adjacency(x, k):
            B, N, _ = x.shape
            x2 = jnp.sum(x * x, axis=-1)
            d2 = x2[:, :, None] + x2[:, None, :] - 2.0 * jnp.einsum('bnc,bmc->bnm', x, x)
            big = jnp.finfo(d2.dtype).max
            d2 = d2 + big * jnp.eye(N, dtype=d2.dtype)
            _, idx = jax.lax.top_k(-d2, k)
            rows = jnp.arange(N)[:, None]

            def scatter_one(idx_b):
                return jnp.zeros((N, N), dtype=bool).at[rows, idx_b].set(True)
            return jax.vmap(scatter_one)(idx)
        key = jax.random.key(seed)
        k1, k2, k3 = jax.random.split(key, 3)
        B, N, C = (2, 2048, 256)
        inner = HEADS * DIM_HEAD
        x = jax.random.normal(k1, (B, N, C), dtype=jnp.float32)
        Wqkv = jax.random.normal(k2, (C, 3 * inner), dtype=jnp.float32) * C ** (-0.5)
        Wout = jax.random.normal(k3, (inner, C), dtype=jnp.float32) * inner ** (-0.5)
        bout = jnp.zeros((C,), dtype=jnp.float32)
        return {'x': x, 'Wqkv': Wqkv, 'Wout': Wout, 'bout': bout}
    _L0_attn_all = _L0_attn_setup()
    _L0_attn_in = {k: v for k, v in _L0_attn_all.items() if k in ('Wqkv', 'Wout', 'bout', )}
    del _L0_attn_all

    def _L0_ffn_setup():
        import jax, jax.numpy as jnp
        import numpy as np
        DIM = 256
        H = 8
        D = 64
        G = 64
        INNER = H * D
        SCALE = D ** (-0.5)
        key = jax.random.key(seed)
        ks = jax.random.split(key, 12)
        B, N = (4, 16384)
        x = jax.random.normal(ks[0], (B, N, DIM), dtype=jnp.float32)
        s = lambda fan_in: 1.0 / np.sqrt(fan_in)
        W_fx = jax.random.normal(ks[1], (DIM, INNER), dtype=jnp.float32) * s(DIM)
        b_fx = jnp.zeros((INNER,), dtype=jnp.float32)
        W_x = jax.random.normal(ks[2], (DIM, INNER), dtype=jnp.float32) * s(DIM)
        b_x = jnp.zeros((INNER,), dtype=jnp.float32)
        A = jax.random.normal(ks[3], (G, D), dtype=jnp.float32)
        Q, _ = jnp.linalg.qr(A.T)
        W_slice = Q[:, :G].astype(jnp.float32)
        b_slice = jnp.zeros((G,), dtype=jnp.float32)
        W_q = jax.random.normal(ks[4], (D, D), dtype=jnp.float32) * s(D)
        W_k = jax.random.normal(ks[5], (D, D), dtype=jnp.float32) * s(D)
        W_v = jax.random.normal(ks[6], (D, D), dtype=jnp.float32) * s(D)
        W_out = jax.random.normal(ks[7], (INNER, DIM), dtype=jnp.float32) * s(INNER)
        b_out = jnp.zeros((DIM,), dtype=jnp.float32)
        temperature = jnp.ones((1, H, 1, 1), dtype=jnp.float32) * 0.5
        return {'x': x, 'W_fx': W_fx, 'b_fx': b_fx, 'W_x': W_x, 'b_x': b_x, 'W_slice': W_slice, 'b_slice': b_slice, 'W_q': W_q, 'W_k': W_k, 'W_v': W_v, 'W_out': W_out, 'b_out': b_out, 'temperature': temperature}
    _L0_ffn_all = _L0_ffn_setup()
    _L0_ffn_in = {k: v for k, v in _L0_ffn_all.items() if k in ('W_fx', 'b_fx', 'W_x', 'b_x', 'W_slice', 'b_slice', 'W_q', 'W_k', 'W_v', 'W_out', 'b_out', 'temperature', )}
    del _L0_ffn_all

    return {
        "x": x,
        "L0_tok_W": _L0_tok_in["W"],
        "L0_tok_b": _L0_tok_in["b"],
        "L0_attn_Wqkv": _L0_attn_in["Wqkv"],
        "L0_attn_Wout": _L0_attn_in["Wout"],
        "L0_attn_bout": _L0_attn_in["bout"],
        "L0_ffn_W_fx": _L0_ffn_in["W_fx"],
        "L0_ffn_b_fx": _L0_ffn_in["b_fx"],
        "L0_ffn_W_x": _L0_ffn_in["W_x"],
        "L0_ffn_b_x": _L0_ffn_in["b_x"],
        "L0_ffn_W_slice": _L0_ffn_in["W_slice"],
        "L0_ffn_b_slice": _L0_ffn_in["b_slice"],
        "L0_ffn_W_q": _L0_ffn_in["W_q"],
        "L0_ffn_W_k": _L0_ffn_in["W_k"],
        "L0_ffn_W_v": _L0_ffn_in["W_v"],
        "L0_ffn_W_out": _L0_ffn_in["W_out"],
        "L0_ffn_b_out": _L0_ffn_in["b_out"],
        "L0_ffn_temperature": _L0_ffn_in["temperature"],
    }

def reference(x, L0_tok_W, L0_tok_b, L0_attn_Wqkv, L0_attn_Wout, L0_attn_bout, L0_ffn_W_fx, L0_ffn_b_fx, L0_ffn_W_x, L0_ffn_b_x, L0_ffn_W_slice, L0_ffn_b_slice, L0_ffn_W_q, L0_ffn_W_k, L0_ffn_W_v, L0_ffn_W_out, L0_ffn_b_out, L0_ffn_temperature):
    import jax
    import jax.numpy as jnp
    def _L0_tok_ref(x, W, b):
        import jax, jax.numpy as jnp
        import numpy as np
        PATCH = 16
        B, C, H, Wd = x.shape
        p = PATCH
        nH, nW = (H // p, Wd // p)
        patches = x.reshape(B, C, nH, p, nW, p)
        patches = patches.transpose(0, 2, 4, 1, 3, 5)
        patches = patches.reshape(B, nH * nW, C * p * p)
        return jnp.einsum('bnk,ek->bne', patches, W) + b

    def _L0_attn_ref(x, Wqkv, Wout, bout):
        import jax, jax.numpy as jnp
        import numpy as np
        HEADS = 8
        DIM_HEAD = 64
        KNN = 32
        SCALE = DIM_HEAD ** (-0.5)

        def _knn_adjacency(x, k):
            B, N, _ = x.shape
            x2 = jnp.sum(x * x, axis=-1)
            d2 = x2[:, :, None] + x2[:, None, :] - 2.0 * jnp.einsum('bnc,bmc->bnm', x, x)
            big = jnp.finfo(d2.dtype).max
            d2 = d2 + big * jnp.eye(N, dtype=d2.dtype)
            _, idx = jax.lax.top_k(-d2, k)
            rows = jnp.arange(N)[:, None]

            def scatter_one(idx_b):
                return jnp.zeros((N, N), dtype=bool).at[rows, idx_b].set(True)
            return jax.vmap(scatter_one)(idx)
        B, N, C = x.shape
        adj = _knn_adjacency(x, KNN)
        qkv = x @ Wqkv
        q, k, v = jnp.split(qkv, 3, axis=-1)
        split_heads = lambda t: t.reshape(B, N, HEADS, DIM_HEAD).transpose(0, 2, 1, 3)
        q, k, v = (split_heads(q), split_heads(k), split_heads(v))
        dots = jnp.einsum('bhnd,bhmd->bhnm', q, k) * SCALE
        dots = jnp.where(adj[:, None, :, :], dots, -jnp.inf)
        attn = jax.nn.softmax(dots, axis=-1)
        out = jnp.einsum('bhnm,bhmd->bhnd', attn, v)
        out = out.transpose(0, 2, 1, 3).reshape(B, N, HEADS * DIM_HEAD)
        return out @ Wout + bout

    def _L0_ffn_ref(x, W_fx, b_fx, W_x, b_x, W_slice, b_slice, W_q, W_k, W_v, W_out, b_out, temperature):
        import jax, jax.numpy as jnp
        import numpy as np
        DIM = 256
        H = 8
        D = 64
        G = 64
        INNER = H * D
        SCALE = D ** (-0.5)
        B, N, _ = x.shape
        fx_mid = (x @ W_fx + b_fx).reshape(B, N, H, D).transpose(0, 2, 1, 3)
        x_mid = (x @ W_x + b_x).reshape(B, N, H, D).transpose(0, 2, 1, 3)
        temp = jnp.clip(temperature, 0.1, 5.0)
        slice_weights = jax.nn.softmax((x_mid @ W_slice + b_slice) / temp, axis=-1)
        slice_norm = slice_weights.sum(axis=2)
        slice_token = jnp.einsum('bhnc,bhng->bhgc', fx_mid, slice_weights)
        slice_token = slice_token / (slice_norm[..., None] + 1e-05)
        q = slice_token @ W_q
        k = slice_token @ W_k
        v = slice_token @ W_v
        attn = jax.nn.softmax(jnp.einsum('bhgc,bhkc->bhgk', q, k) * SCALE, axis=-1)
        out_slice = jnp.einsum('bhgk,bhkc->bhgc', attn, v)
        out_x = jnp.einsum('bhgc,bhng->bhnc', out_slice, slice_weights)
        out_x = out_x.transpose(0, 2, 1, 3).reshape(B, N, INNER)
        return out_x @ W_out + b_out

    h = _L0_tok_ref(x, L0_tok_W, L0_tok_b)
    h = h + _L0_attn_ref(_layernorm(h, axis=-1), L0_attn_Wqkv, L0_attn_Wout, L0_attn_bout)
    h = h + _L0_ffn_ref(_layernorm(h, axis=-1), L0_ffn_W_fx, L0_ffn_b_fx, L0_ffn_W_x, L0_ffn_b_x, L0_ffn_W_slice, L0_ffn_b_slice, L0_ffn_W_q, L0_ffn_W_k, L0_ffn_W_v, L0_ffn_W_out, L0_ffn_b_out, L0_ffn_temperature)
    return h


_drawn_inputs = setup_inputs


def setup_inputs(seed=0):
    import zlib

    import numpy as np

    out = dict(_drawn_inputs(seed))
    spreads = {'L0_attn_bout': (0.0, 0.1),
     'L0_ffn_b_fx': (0.0, 0.1),
     'L0_ffn_b_x': (0.0, 0.8),
     'L0_ffn_b_slice': (0.0, 0.8),
     'L0_ffn_b_out': (0.0, 0.1),
     'L0_ffn_temperature': (0.5, 0.6)}
    factors = {'L0_ffn_W_x': 6.129, 'L0_ffn_W_slice': 7.169, 'L0_ffn_W_q': 8.0, 'L0_ffn_W_k': 8.0}
    for name, (base, spread) in spreads.items():
        noise = np.random.default_rng([zlib.crc32(name.encode()), seed]).standard_normal(out[name].shape)
        drawn = base * np.exp(spread * noise) if base else spread * noise
        out[name] = jnp.asarray(drawn.astype(out[name].dtype))
    for name, factor in factors.items():
        out[name] = (out[name] * factor).astype(out[name].dtype)
    return out
```

```python
import concourse.bass as bass
from concourse import mybir
from contextlib import ExitStack


BATCH, CHANNELS, SIDE, PATCH = 32, 3, 336, 16
GRID = SIDE // PATCH
TOKENS = GRID * GRID
E = 256
PATCH_K = CHANNELS * PATCH * PATCH
HEADS, DH, KNN = 8, 64, 32
SLICES = 64
INNER = HEADS * DH
P = 128
ROWS = 112
NT = 4
NP = ROWS * NT
LAST = TOKENS - (NT - 1) * ROWS
KT = PATCH_K // P
EC = E // P
PAIRS = HEADS // 2
MAXROWS = 2 * HEADS
VW = DH + 1
SCALE = DH ** -0.5
EPS = 1e-5
OFF = -1e30
DIAG = -1e36
TAKEN = -3e38
TAKEN_BELOW = -2e38
assert MAXROWS + ROWS == P


class Image:

    def __init__(self, reg, off):
        self.reg, self.off = reg, off

    def count(self, per, k):
        c = self.off * per + k
        return c if self.reg is None else self.reg * (2 * per) + c

    def index(self):
        return self.off if self.reg is None else self.reg * 2 + self.off

    def back(self, n):
        return Image(self.reg, self.off - n)

    def exists(self):
        return self.reg is not None or self.off >= 0


class Ring:

    def __init__(self, banks, full, free, slots):
        self.banks, self.full, self.free = banks, full, free
        self.place, self.per = {}, [0] * len(banks)
        for n, name in enumerate(slots):
            b = n % len(banks)
            self.place[name] = (b, self.per[b])
            self.per[b] += 1

    def bank(self, name):
        return self.banks[self.place[name][0]]

    def full_of(self, name):
        return self.full[self.place[name][0]]

    def free_of(self, name):
        return self.free[self.place[name][0]]

    def emptied(self, name, img):
        b, k = self.place[name]
        return self.free[b], img.count(self.per[b], k)

    def holds(self, name, img):
        b, k = self.place[name]
        return self.full[b], img.count(self.per[b], k + 1)

    def gone(self, name, img):
        b, k = self.place[name]
        return self.free[b], img.count(self.per[b], k + 1)

    def all_gone(self, names, img):
        last = {}
        for name in sorted(names, key=lambda x: self.place[x][1]):
            last[self.place[name][0]] = name
        return [self.gone(name, img) for name in last.values()]


class Steps:

    def __init__(self, per):
        self.per, self.img, self.k = per, None, 0

    def begin(self, img):
        assert self.k in (0, self.per), (self.k, self.per)
        self.img, self.k = img, 0

    def next(self):
        self.k += 1
        return self.img.count(self.per, self.k)


def build(nc, xt, wtok, btok, wqkv, wout, bout, wfx, bfx, wxT, bx, wslice, bslice, temp,
          wq2, wk2, wv2, wout2, bout2, identf, identb, diag, pick, out):
    fp32, bf16 = mybir.dt.float32, mybir.dt.bfloat16
    ALU, ACT, AX = mybir.AluOpType, mybir.ActivationFunctionType, mybir.AxisListType.X

    ctx = ExitStack()
    with ctx:
        def sb(name, shape, dt=fp32):
            return ctx.enter_context(nc.sbuf_tensor(name, shape, dt))

        def sem(name):
            return ctx.enter_context(nc.semaphore(name))

        consts = []

        def const(name, dram, dt=fp32):
            t = sb(name, list(dram.shape), dt)
            consts.append((t, dram))
            return t

        wtok_s = const("wtok_s", wtok)
        btok_s = const("btok_s", btok)
        wqkv_s = const("wqkv_s", wqkv)
        wout_s = const("wout_s", wout)
        bout_s = const("bout_s", bout)
        wfx_s = const("wfx_s", wfx)
        bfx_s = const("bfx_s", bfx)
        bx_s = const("bx_s", bx)
        wslice_s = const("wslice_s", wslice)
        temp_s = const("temp_s", temp)
        wq2_s = const("wq2_s", wq2)
        wk2_s = const("wk2_s", wk2)
        wv2_s = const("wv2_s", wv2)
        wout2_s = const("wout2_s", wout2)
        bout2_s = const("bout2_s", bout2)
        identf_s = const("identf_s", identf)
        identb_s = const("identb_s", identb, bf16)
        diag_s = const("diag_s", diag, bf16)
        pick_s = const("pick_s", pick, bf16)
        ones_s = sb("ones_s", [P, P])
        half_s = sb("half_s", [P, NT])
        eps_s = sb("eps_s", [P, NT])
        wlog_s = sb("wlog_s", [P, EC, INNER])
        blog_s = sb("blog_s", [P, INNER])

        patches = sb("patches", [P, KT, NP])
        h = [sb(f"h{b}", [P, NT, E]) for b in range(2)]
        bn1 = sb("bn1", [P, NT, 6])
        mv1 = sb("mv1", [P, NT, 2])
        ve1 = sb("ve1", [P, NT])
        rstd1 = sb("rstd1", [P, NT])
        z = sb("z", [P, NT, E])
        zT = sb("zT", [P, EC, NP])
        early = sb("early", [P, 1024])
        zsq = early[:, 0:EC * NP].rearrange("p (c n) -> p c n", c=EC)
        x2 = sb("x2", [P, NP])
        scorebuf = sb("scorebuf", [P, NT * NP])
        score = scorebuf[:, :].rearrange("p (t n) -> p t n", t=NT)
        top8 = sb("top8", [P, NT, 8])
        mask = [sb(f"mask{b}", [P, NT, MAXROWS + NP], bf16) for b in range(2)]
        maskmax = [sb(f"maskmax{b}", [P, NT, NP], bf16) for b in range(2)]
        qT = [sb(f"qT{b}", [P, PAIRS, NP]) for b in range(2)]
        kT = [sb(f"kT{b}", [P, PAIRS, NP]) for b in range(2)]
        v = [sb(f"v{b}", [P, NT, HEADS, VW]) for b in range(2)]

        junk = [sb(f"junk{b}", [P, NP], bf16) for b in range(3)]
        mx = sb("mx", [P, NT, HEADS])
        maxhl = sb("maxhl", [P, NT, MAXROWS], bf16)
        heads = [sb(f"heads{b}", [P, NT * INNER]) for b in range(2)]
        probs = [x[:, 0:NT * NP].rearrange("p (t n) -> p t n", t=NT) for x in heads]
        rden = sb("rden", [P, HEADS, NT])
        mid = sb("mid", [P, NT * INNER])
        o = mid[:, :].rearrange("p (t n) -> p t n", t=NT)
        oT = sb("oT", [P, PAIRS, NP])
        h2 = sb("h2", [P, NT, E])
        bn2 = sb("bn2", [P, NT, 6])
        mv2 = sb("mv2", [P, NT, 2])
        ve2 = sb("ve2", [P, NT])
        rstd2 = sb("rstd2", [P, NT])
        z2, z2T = z, zsq
        fx = sb("fx", [P, NT, PAIRS, P + 1])
        logit, sw = [x[:, :].rearrange("p (t h g) -> p t h g", t=NT, h=HEADS) for x in heads]
        lmax = sb("lmax", [P, NT, HEADS])
        lsum = sb("lsum", [P, NT, HEADS])
        swT = oT
        snorm = sb("snorm", [P, PAIRS])
        token = sb("token", [P, PAIRS, P])
        tokenT, q2, v2, attnT = [mid[:, n * 512:(n + 1) * 512].rearrange("p (c k) -> p c k", c=PAIRS) for n in range(4)]
        k2 = sb("k2", [P, PAIRS, SLICES])
        amax = sb("amax", [P, PAIRS])
        ash = sb("ash", [P, PAIRS, SLICES])
        aexp = sb("aexp", [P, PAIRS, SLICES])
        asum = sb("asum", [P, PAIRS])
        attn = sb("attn", [P, PAIRS, P])
        u = early[:, :].rearrange("p (c e) -> p c e", c=PAIRS)
        mix = scorebuf[:, 0:PAIRS * E].rearrange("p (c e) -> p c e", c=PAIRS)
        res = sb("res", [P, NT, E])
        wxT_s = res[:, :, :]
        bslice_s = z[:, 0:2, :].rearrange("p a b -> p (a b)")
        bxrep = heads[0][:, 0:PAIRS * P].rearrange("p (c k) -> p c k", c=PAIRS)
        consts += [(wxT_s, wxT), (bslice_s, bslice)]

        def ring(name, n, slots):
            banks = [ctx.enter_context(nc.psum_tensor(f"{name}{b}", [P, 512], fp32)) for b in range(n)]
            return Ring(banks, [sem(f"{name}{b}_full") for b in range(n)],
                        [sem(f"{name}{b}_free") for b in range(n)], slots)

        T4, C4, H8 = range(NT), range(PAIRS), range(HEADS)
        front = ring("front", 2, [f"tok{t}" for t in T4] + ["zT0", "zT1", "x2"] + [f"gram{t}" for t in T4]
                     + [f"q{c}" for c in C4] + [f"k{c}" for c in C4] + [f"v{t}" for t in T4]
                     + [f"maskT{t}" for t in T4])
        scores = ring("scores", 3, [f"s{t}_{hd}" for t in T4 for hd in H8]
                      + [f"sT{hd}_{t}" for hd in H8 for t in T4])
        rest = ring("rest", 3, ["maxT"] + [f"pv{hd}" for hd in H8] + [f"oT{c}" for c in C4]
                    + [f"proj{t}" for t in T4] + ["z2T0", "z2T1"] + [f"fx{t}" for t in T4]
                    + [f"logit{t}" for t in T4] + [f"swT{c}" for c in C4] + ["token0", "token1", "tokenT",
                    "q2", "k2", "v2", "s2", "u0", "u1", "attnT", "mix0", "mix1"]
                    + [f"out{t}" for t in T4])

        consts_in = sem("consts_in")
        setup_vec = sem("setup_vec")
        setup_chain = sem("setup_chain")
        setup_pe = sem("setup_pe")
        patches_in = sem("patches_in")
        out_stored = sem("out_stored")
        var1_ready = sem("var1_ready")
        var2_ready = sem("var2_ready")
        rstd1_ready = sem("rstd1_ready")
        rstd2_ready = sem("rstd2_ready")
        z_ready = sem("z_ready")
        z2_ready = sem("z2_ready")
        h_biased = sem("h_biased")
        h2_biased = sem("h2_biased")
        mask_ready = sem("mask_ready")
        maxhl_ready = sem("maxhl_ready")
        logit_shifted = sem("logit_shifted")
        logit_exped = sem("logit_exped")
        sw_ready = sem("sw_ready")
        attn_exped = sem("attn_exped")
        attn_ready = sem("attn_ready")
        vec_front_step = sem("vec_front_step")
        vec_back_step = sem("vec_back_step")
        pool_root1_step = sem("pool_root1_step")
        pool_root2_step = sem("pool_root2_step")

        block = ctx.enter_context(nc.Block())

        def over_images(eng, back_and_front):
            back_and_front(None, Image(None, 0))
            back_and_front(Image(None, 0), Image(None, 1))
            with eng.Fori(0, BATCH // 2 - 1) as i:
                back_and_front(Image(i, 1), Image(i, 2))
                back_and_front(Image(i, 2), Image(i, 3))
            back_and_front(Image(None, BATCH - 1), None)

        def par(img):
            return img.off % 2

        @block.sync
        def _(sp):
            for t, dram in consts:
                sp.dma_start(t if isinstance(t, bass.AP) else t[:], dram).then_inc(consts_in, 16)

            sp.wait_ge(out_stored, 32 * BATCH)

        @block.tensor
        def _(pe):
            mm = nc.tensor.matmul
            pe.wait_ge(consts_in, 16 * len(consts))
            pe.wait_ge(setup_vec, 2)
            for c in range(EC):
                for p in C4:
                    last = mm(scores.banks[c][:, p * P:(p + 1) * P], wxT_s[:, p, c * P:(c + 1) * P],
                              wslice_s[:, :], start=True, stop=True)
            for p in C4:
                last = mm(scores.banks[2][:, p * P:(p + 1) * P], bxrep[:, p, :], wslice_s[:, :],
                          start=True, stop=True)
            last.then_inc(setup_pe, 1)
            pe.wait_ge(setup_vec, 5)

            def tok(F):
                pe.wait_ge(patches_in, F.count(16, 16))
                for t in T4:
                    pe.wait_ge(*front.emptied(f"tok{t}", F))
                    bank = front.bank(f"tok{t}")
                    for k in range(KT):
                        last = mm(bank[0:ROWS, 0:E], patches[:, k, t * ROWS:(t + 1) * ROWS],
                                  wtok_s[:, k, :], start=(k == 0), stop=(k == KT - 1))
                    last.then_inc(front.full_of(f"tok{t}"), 1)

            def transposes(ring_, names, img, src, ident):
                for c, name in enumerate(names):
                    pe.wait_ge(*ring_.emptied(name, img))
                    bank = ring_.bank(name)
                    for t in T4:
                        last = nc.tensor.transpose(bank[:, t * ROWS:(t + 1) * ROWS],
                                                   src[0:ROWS, t, c * P:(c + 1) * P], ident[0:ROWS, 0:ROWS])
                    last.then_inc(ring_.full_of(name), 1)

            def ztr(F):
                pe.wait_ge(z_ready, F.count(1, 1))
                transposes(front, ["zT0", "zT1"], F, z, identf_s)

            def gram(F):
                for sem_, n in front.all_gone(["zT0", "zT1"], F):
                    pe.wait_ge(sem_, n)
                pe.wait_ge(*front.emptied("x2", F))
                bank = front.bank("x2")
                for c in range(EC):
                    last = mm(bank[0:ROWS, 0:NP], ones_s[:, 0:ROWS], zsq[:, c, :], start=(c == 0), stop=(c == 1))
                last.then_inc(front.full_of("x2"), 1)
                for t in T4:
                    pe.wait_ge(*front.emptied(f"gram{t}", F))
                    bank = front.bank(f"gram{t}")
                    for c in range(EC):
                        mm(bank[0:ROWS, 0:NP], zT[:, c, t * ROWS:(t + 1) * ROWS], zT[:, c, :],
                           start=(c == 0), stop=False)
                    last = mm(bank[0:ROWS, 0:NP], identb_s[0:ROWS, 0:ROWS], diag_s[0:ROWS, t, :],
                              start=False, stop=True)
                    last.then_inc(front.full_of(f"gram{t}"), 1)

            def qk(F, which):
                base = {"q": 0, "k": INNER}[which]
                for p in C4:
                    pe.wait_ge(*front.emptied(f"{which}{p}", F))
                    bank = front.bank(f"{which}{p}")
                    for c in range(EC):
                        last = mm(bank[:, 0:NP], wqkv_s[:, c, base + p * P:base + (p + 1) * P], zT[:, c, :],
                                  start=(c == 0), stop=(c == 1))
                    last.then_inc(front.full_of(f"{which}{p}"), 1)

            def vals(F, ts):
                for t in ts:
                    pe.wait_ge(*front.emptied(f"v{t}", F))
                    bank = front.bank(f"v{t}")
                    for c in range(EC):
                        last = mm(bank[0:ROWS, :], zT[:, c, t * ROWS:(t + 1) * ROWS],
                                  wqkv_s[:, c, 2 * INNER:3 * INNER], start=(c == 0), stop=(c == 1))
                    last.then_inc(front.full_of(f"v{t}"), 1)

            def mask_tr(F, ts):
                pe.wait_ge(mask_ready, F.count(1, 1))
                for mt in ts:
                    pe.wait_ge(*front.emptied(f"maskT{mt}", F))
                    bank = front.bank(f"maskT{mt}").bitcast(bf16)
                    for t in T4:
                        last = nc.tensor.transpose(bank[:, t * ROWS:(t + 1) * ROWS],
                                                   mask[par(F)][0:ROWS, t, mt * ROWS:mt * ROWS + P],
                                                   identb_s[0:ROWS, 0:ROWS])
                    last.then_inc(front.full_of(f"maskT{mt}"), 1)

            def score_rows(B):
                b = par(B)
                for sem_, n in front.all_gone([f"{x}{p}" for x in "qk" for p in C4], B):
                    pe.wait_ge(sem_, n)
                for t in T4:
                    for hd in H8:
                        o_, p = (hd % 2) * DH, hd // 2
                        pe.wait_ge(*scores.emptied(f"s{t}_{hd}", B))
                        bank = scores.bank(f"s{t}_{hd}")
                        mm(bank[0:ROWS, 0:NP], qT[b][o_:o_ + DH, p, t * ROWS:(t + 1) * ROWS],
                                         kT[b][o_:o_ + DH, p, :], start=True, stop=True).then_inc(scores.full_of(f"s{t}_{hd}"), 1)

            def max_tr(B):
                pe.wait_ge(maxhl_ready, B.count(1, 1))
                pe.wait_ge(*rest.emptied("maxT", B))
                bank = rest.bank("maxT").bitcast(bf16)
                for t in T4:
                    last = nc.tensor.transpose(bank[0:MAXROWS, t * ROWS:(t + 1) * ROWS],
                                               maxhl[0:ROWS, t, :], identb_s[0:ROWS, 0:ROWS])
                last.then_inc(rest.full_of("maxT"), 1)

            def score_cols(B, hd):
                b = par(B)
                o_, p = (hd % 2) * DH, hd // 2
                if hd == 0:
                    for sem_, n in front.all_gone([f"maskT{t}" for t in T4], B):
                        pe.wait_ge(sem_, n)
                    pe.wait_ge(*rest.gone("maxT", B))
                for t in T4:
                    pe.wait_ge(*scores.emptied(f"sT{hd}_{t}", B))
                    bank = scores.bank(f"sT{hd}_{t}")
                    mm(bank[0:ROWS, 0:NP], kT[b][o_:o_ + DH, p, t * ROWS:(t + 1) * ROWS],
                       qT[b][o_:o_ + DH, p, :], start=True, stop=False)
                    last = mm(bank[0:ROWS, 0:NP], pick_s[:, hd, :], maskmax[b][:, t, :], start=False, stop=True)
                    last.then_inc(scores.full_of(f"sT{hd}_{t}"), 1)

            def pv(B, hd):
                b = par(B)
                if hd == 0:
                    for sem_, n in front.all_gone([f"v{t}" for t in T4], B):
                        pe.wait_ge(sem_, n)
                for sem_, n in scores.all_gone([f"sT{hd}_{t}" for t in T4], B):
                    pe.wait_ge(sem_, n)
                pe.wait_ge(*rest.emptied(f"pv{hd}", B))
                bank = rest.bank(f"pv{hd}")
                for t in T4:
                    for m in T4:
                        last = mm(bank[0:ROWS, t * VW:(t + 1) * VW], probs[hd % 2][0:ROWS, m, t * ROWS:(t + 1) * ROWS],
                                  v[b][0:ROWS, m, hd, :], start=(m == 0), stop=(m == NT - 1))
                last.then_inc(rest.full_of(f"pv{hd}"), 1)

            def rows_product(B, names, srcT, w, n):
                chunks = srcT.shape[1]
                for t in T4:
                    pe.wait_ge(*rest.emptied(names[t], B))
                    bank = rest.bank(names[t])
                    for c in range(chunks):
                        last = mm(bank[0:ROWS, 0:n], srcT[:, c, t * ROWS:(t + 1) * ROWS], w[:, c, :],
                                  start=(c == 0), stop=(c == chunks - 1))
                    last.then_inc(rest.full_of(names[t]), 1)

            def o_and_proj(B):
                for sem_, n in rest.all_gone([f"pv{hd}" for hd in H8], B):
                    pe.wait_ge(sem_, n)
                transposes(rest, [f"oT{c}" for c in C4], B, o, identf_s)
                for sem_, n in rest.all_gone([f"oT{c}" for c in C4], B):
                    pe.wait_ge(sem_, n)
                rows_product(B, [f"proj{t}" for t in T4], oT, wout_s, E)

            def ffn_in(B):
                pe.wait_ge(z2_ready, B.count(1, 1))
                transposes(rest, ["z2T0", "z2T1"], B, z2, identf_s)
                for sem_, n in rest.all_gone(["z2T0", "z2T1"], B):
                    pe.wait_ge(sem_, n)
                rows_product(B, [f"fx{t}" for t in T4], z2T, wfx_s, INNER)
                rows_product(B, [f"logit{t}" for t in T4], z2T, wlog_s, INNER)

            def sw_tr(B):
                pe.wait_ge(sw_ready, B.count(NT, NT))
                for c in C4:
                    pe.wait_ge(*rest.emptied(f"swT{c}", B))
                    bank = rest.bank(f"swT{c}")
                    for t in T4:
                        last = nc.tensor.transpose(bank[:, t * ROWS:(t + 1) * ROWS],
                                                   sw[0:ROWS, t, 2 * c:2 * c + 2, :], identf_s[0:ROWS, 0:ROWS])
                    last.then_inc(rest.full_of(f"swT{c}"), 1)

            def tokens(B):
                for sem_, n in rest.all_gone(["swT1", *[f"fx{t}" for t in T4]], B):
                    pe.wait_ge(sem_, n)
                for g in range(2):
                    pe.wait_ge(*rest.emptied(f"token{g}", B))
                    bank = rest.bank(f"token{g}")
                    for j in range(2):
                        p = 2 * g + j
                        for t in T4:
                            n = ROWS if t < NT - 1 else LAST
                            last = mm(bank[:, j * (P + 1):(j + 1) * (P + 1)], sw[0:n, t, 2 * p:2 * p + 2, :],
                                      fx[0:n, t, p, :], start=(t == 0), stop=(t == NT - 1))
                    last.then_inc(rest.full_of(f"token{g}"), 1)

            def square_tr(B, src, name):
                pe.wait_ge(*rest.emptied(name, B))
                bank = rest.bank(name)
                for p in C4:
                    last = nc.tensor.transpose(bank[:, p * P:(p + 1) * P], src[:, p, :], identf_s[:])
                last.then_inc(rest.full_of(name), 1)

            def token_tr(B):
                for sem_, n in rest.all_gone(["token0", "token1"], B):
                    pe.wait_ge(sem_, n)
                square_tr(B, token, "tokenT")

            def token_qkv(B):
                pe.wait_ge(*rest.gone("tokenT", B))
                for name, w in (("q2", wq2_s), ("k2", wk2_s), ("v2", wv2_s)):
                    pe.wait_ge(*rest.emptied(name, B))
                    bank = rest.bank(name)
                    mm(bank[:, :], w[:], tokenT[:, :, :], start=True, stop=True).then_inc(rest.full_of(name), 1)

            def token_scores(B):
                for sem_, n in rest.all_gone(["q2", "k2"], B):
                    pe.wait_ge(sem_, n)
                pe.wait_ge(*rest.emptied("s2", B))
                bank = rest.bank("s2")
                for p in C4:
                    last = mm(bank[:, p * SLICES:(p + 1) * SLICES], q2[:, p, :], k2[:, p, :], start=True, stop=True)
                last.then_inc(rest.full_of("s2"), 1)

            def paired(B, names, lhs, rhs):
                for g in range(2):
                    pe.wait_ge(*rest.emptied(names[g], B))
                    bank = rest.bank(names[g])
                    for j in range(2):
                        p = 2 * g + j
                        last = mm(bank[:, j * E:(j + 1) * E], lhs[:, p, :], rhs[:, p, :], start=True, stop=True)
                    last.then_inc(rest.full_of(names[g]), 1)

            def body(B, F):
                if B is not None:
                    score_rows(B)
                if F is not None:
                    tok(F)
                if B is not None:
                    max_tr(B)
                    score_cols(B, 0)
                    score_cols(B, 1)
                    pv(B, 0)
                if F is not None:
                    ztr(F)
                if B is not None:
                    score_cols(B, 2)
                    pv(B, 1)
                if F is not None:
                    gram(F)
                if B is not None:
                    for hd in range(3, HEADS):
                        score_cols(B, hd)
                        pv(B, hd - 1)
                    pv(B, HEADS - 1)
                    o_and_proj(B)
                if F is not None:
                    qk(F, "q")
                if B is not None:
                    ffn_in(B)
                if F is not None:
                    qk(F, "k")
                if B is not None:
                    sw_tr(B)
                    tokens(B)
                if F is not None:
                    vals(F, [0, 1])
                if B is not None:
                    token_tr(B)
                if F is not None:
                    vals(F, [2])
                if B is not None:
                    token_qkv(B)
                if F is not None:
                    vals(F, [3])
                if B is not None:
                    token_scores(B)
                    pe.wait_ge(*rest.gone("v2", B))
                    paired(B, ["u0", "u1"], v2, wout2_s)
                if F is not None:
                    mask_tr(F, T4)
                if B is not None:
                    pe.wait_ge(attn_ready, B.count(1, 1))
                    square_tr(B, attn, "attnT")
                    for sem_, n in rest.all_gone(["attnT", "u0", "u1"], B):
                        pe.wait_ge(sem_, n)
                    paired(B, ["mix0", "mix1"], attnT, u)
                    for sem_, n in rest.all_gone(["mix0", "mix1", "attnT", *[f"swT{c}" for c in C4]], B):
                        pe.wait_ge(sem_, n)
                    rows_product(B, [f"out{t}" for t in T4], swT, mix, E)

            over_images(pe, body)

        @block.scalar
        def _(act):
            def copy(ring_, name, img, dst, width=None, src=None):
                act.wait_ge(*ring_.holds(name, img))
                bank = ring_.bank(name)
                nc.scalar.activation(dst, bank[:, 0:width] if src is None else src(bank), ACT.Copy).then_inc(ring_.free_of(name), 1)

            def front_transposed(F):
                for c in range(EC):
                    act.wait_ge(*front.holds(f"zT{c}", F))
                    bank = front.bank(f"zT{c}")
                    nc.scalar.activation(zsq[:, c, :], bank[:, 0:NP], ACT.Square)
                    nc.scalar.activation(zT[:, c, :], bank[:, 0:NP], ACT.Copy).then_inc(front.free_of(f"zT{c}"), 1)

            def norms(F):
                act.wait_ge(*front.holds("x2", F))
                bank = front.bank("x2")
                if F.back(1).exists():
                    act.wait_ge(*front.gone("gram3", F.back(1)))
                nc.scalar.activation(x2[0:ROWS, :], bank[0:ROWS, 0:NP], ACT.Copy).then_inc(front.free_of("x2"), 1)

            def qk(F, which):
                dst = {"q": qT, "k": kT}[which][par(F)]
                for p in C4:
                    copy(front, f"{which}{p}", F, dst[:, p, :], NP)

            def vals(F, ts):
                for t in ts:
                    copy(front, f"v{t}", F, v[par(F)][0:ROWS, t, :, 0:DH],
                         src=lambda bank: bank[0:ROWS, :].rearrange("p (h d) -> p h d", h=HEADS))

            def masks(F):
                for t in T4:
                    copy(front, f"maskT{t}", F, maskmax[par(F)][:, t, :],
                         src=lambda bank: bank.bitcast(bf16)[:, 0:NP])

            def maxima(B):
                act.wait_ge(*rest.holds("maxT", B))
                bank = rest.bank("maxT")
                for t in T4:
                    last = nc.scalar.activation(maskmax[par(B)][0:MAXROWS, t, :],
                                                bank.bitcast(bf16)[0:MAXROWS, 0:NP], ACT.Copy)
                last.then_inc(rest.free_of("maxT"), 1)

            def exps(B, hd):
                for t in T4:
                    act.wait_ge(*scores.holds(f"sT{hd}_{t}", B))
                    bank = scores.bank(f"sT{hd}_{t}")
                    nc.scalar.activation(probs[hd % 2][0:ROWS, t, :], bank[0:ROWS, 0:NP],
                                                        ACT.Exp, scale=SCALE).then_inc(scores.free_of(f"sT{hd}_{t}"), 1)

            def load(F):
                if F.back(1).exists():
                    act.wait_ge(*front.holds("tok3", F.back(1)))
                act.dma_start(patches[:], xt[F.index()]).then_inc(patches_in, 16)

            def store(B):
                for sem_, n in rest.all_gone([f"out{t}" for t in T4], B):
                    act.wait_ge(sem_, n)
                n = B.index()
                act.dma_start(out[n, 0:3 * ROWS, :].rearrange("(t p) e -> p t e", p=ROWS),
                              res[0:ROWS, 0:3, :]).then_inc(out_stored, 16)
                act.dma_start(out[n, 3 * ROWS:TOKENS, :], res[0:LAST, 3, :]).then_inc(out_stored, 16)

            def body(B, F):
                if F is not None:
                    load(F)
                if B is not None:
                    maxima(B)
                    exps(B, 0)
                    exps(B, 1)
                if F is not None:
                    front_transposed(F)
                if B is not None:
                    exps(B, 2)
                if F is not None:
                    norms(F)
                if B is not None:
                    for hd in range(3, HEADS):
                        exps(B, hd)
                    for c in C4:
                        copy(rest, f"oT{c}", B, oT[:, c, :], NP)
                if F is not None:
                    qk(F, "q")
                if B is not None:
                    for c in range(EC):
                        copy(rest, f"z2T{c}", B, z2T[:, c, :], NP)
                if F is not None:
                    qk(F, "k")
                if B is not None:
                    for t in T4:
                        act.wait_ge(logit_shifted, B.count(NT, t + 1))
                        nc.scalar.activation(sw[0:ROWS, t, :, :], logit[0:ROWS, t, :, :], ACT.Exp)\
                          .then_inc(logit_exped, 1)
                    for c in C4:
                        copy(rest, f"swT{c}", B, swT[:, c, :], NP)
                if F is not None:
                    vals(F, [0, 1])
                if B is not None:
                    copy(rest, "tokenT", B, tokenT[:, :, :], 512)
                if F is not None:
                    vals(F, [2])
                if B is not None:
                    copy(rest, "q2", B, q2[:, :, :], 512)
                    act.wait_ge(*rest.holds("k2", B))
                    bank = rest.bank("k2")
                    v4 = bank[:, :].rearrange("p (c k) -> p c k", c=PAIRS)
                    nc.scalar.activation(k2[0:DH, :, :], v4[0:DH, :, 0:SLICES], ACT.Copy)
                    nc.scalar.activation(k2[DH:P, :, :], v4[DH:P, :, SLICES:P], ACT.Copy).then_inc(rest.free_of("k2"), 1)
                    copy(rest, "v2", B, v2[:, :, :], 512)
                if F is not None:
                    vals(F, [3])
                if B is not None:
                    act.wait_ge(*rest.gone("s2", B))
                    nc.scalar.activation(aexp[:, :, :], ash[:, :, :], ACT.Exp, scale=SCALE)\
                      .then_inc(attn_exped, 1)
                    for g in range(2):
                        copy(rest, f"u{g}", B, u[:, 2 * g:2 * g + 2, :], 512)
                if F is not None:
                    masks(F)
                if B is not None:
                    copy(rest, "attnT", B, attnT[:, :, :], 512)
                    for g in range(2):
                        copy(rest, f"mix{g}", B, mix[:, 2 * g:2 * g + 2, :], 512)
                    store(B)

            over_images(act, body)

        @block.vector
        def _(dve):
            V = nc.vector

            def take_wait():
                dve.nop(nofuse=True)

            back_step = Steps(1 + HEADS + 1 + 3 * NT + 4 + 3)
            front_step = Steps(1 + 8 * NT)

            V.memset(ones_s[:], 1.0)
            V.memset(half_s[:], -0.5)
            V.memset(eps_s[:], EPS)
            for b in range(2):
                V.memset(mask[b][:, :, 0:MAXROWS], 0.0)
                V.memset(v[b][:, :, :, DH:VW], 1.0)
            V.memset(fx[:, :, :, P:P + 1], 1.0)
            V.memset(token[:], 0.0)
            V.memset(attn[:], 0.0).then_inc(setup_vec, 1)
            dve.wait_ge(consts_in, 16 * len(consts))
            V.tensor_scalar(temp_s[:], temp_s[:], 0.1, 5.0, ALU.max, ALU.min).then_inc(setup_chain, 1)
            V.tensor_copy(bxrep, bx_s[:, :].unsqueeze(2).to_broadcast([P, PAIRS, P])).then_inc(setup_vec, 1)
            dve.wait_ge(setup_chain, 1)
            V.reciprocal(temp_s[:], temp_s[:]).then_inc(setup_chain, 1)
            dve.wait_ge(setup_chain, 2)
            invt = temp_s[:, :].unsqueeze(2).to_broadcast([P, HEADS, SLICES])
            dve.wait_ge(setup_pe, 1)
            for c in range(EC):
                V.tensor_tensor(wlog_s[:, c, :].rearrange("p (h g) -> p h g", h=HEADS),
                                scores.banks[c][:, :].rearrange("p (h g) -> p h g", h=HEADS),
                                invt, ALU.mult).then_inc(setup_vec, 1)
            V.tensor_tensor(blog_s[:], scores.banks[2][:, :], bslice_s, ALU.add).then_inc(setup_chain, 1)
            dve.wait_ge(setup_chain, 3)
            V.tensor_tensor(blog_s[:, :].rearrange("p (h g) -> p h g", h=HEADS),
                            blog_s[:, :].rearrange("p (h g) -> p h g", h=HEADS), invt, ALU.mult)\
             .then_inc(setup_vec, 1)
            dve.wait_ge(setup_vec, 5)

            def layernorm(steps, step_sem, img, src, bn, mv, dst, var_sem, rstd, rstd_sem, dst_sem):
                for t in T4:
                    last = V.bn_stats(bn[0:ROWS, t, :], src[0:ROWS, t, :])
                last.then_inc(step_sem, 1)
                dve.wait_ge(step_sem, steps.next())
                take_wait()
                for t in T4:
                    last = V.bn_aggr(mv[0:ROWS, t, :], bn[0:ROWS, t, :])
                last.then_inc(var_sem, 1)
                dve.wait_ge(rstd_sem, img.count(1, 1))
                for t in T4:
                    last = V.tensor_scalar(dst[0:ROWS, t, :], src[0:ROWS, t, :], mv[0:ROWS, t, 0:1],
                                           rstd[0:ROWS, t:t + 1], ALU.subtract, ALU.mult)
                last.then_inc(dst_sem, 1)

            def tok(F):
                front_step.begin(F)
                for t in T4:
                    dve.wait_ge(*front.holds(f"tok{t}", F))
                    bank = front.bank(f"tok{t}")
                    V.tensor_tensor(h[par(F)][0:ROWS, t, :], bank[0:ROWS, 0:E],
                                                  btok_s[0:ROWS, :], ALU.add).then_inc(front.free_of(f"tok{t}"), 1)
                for sem_, n in front.all_gone([f"tok{t}" for t in T4], F):
                    dve.wait_ge(sem_, n)
                layernorm(front_step, vec_front_step, F, h[par(F)], bn1, mv1, z, var1_ready, rstd1, rstd1_ready, z_ready)

            def gram(F):
                dve.wait_ge(*front.gone("x2", F))
                for t in T4:
                    dve.wait_ge(*front.holds(f"gram{t}", F))
                    bank = front.bank(f"gram{t}")
                    V.scalar_tensor_tensor(out=score[0:ROWS, t, :], in0=bank[0:ROWS, 0:NP],
                                                         scalar=2.0, in1=x2[0:ROWS, :], op0=ALU.mult,
                                                         op1=ALU.subtract).then_inc(front.free_of(f"gram{t}"), 1)

            def neighbours(F, t):
                dve.wait_ge(*front.gone(f"gram{t}", F))
                row = score[0:ROWS, t, :]
                for r in range(KNN // 8):
                    take_wait()
                    V.max(out=top8[0:ROWS, t, :], in_=row).then_inc(vec_front_step, 1)
                    dve.wait_ge(vec_front_step, front_step.next())
                    take_wait()
                    V.match_replace(out=row, in_to_replace=top8[0:ROWS, t, :], in_values=row,
                                                     imm_value=TAKEN).then_inc(vec_front_step, 1)
                    dve.wait_ge(vec_front_step, front_step.next())
                last = V.tensor_scalar(mask[par(F)][0:ROWS, t, MAXROWS:], row, TAKEN_BELOW, OFF, ALU.is_gt, ALU.mult)
                if t == NT - 1:
                    last.then_inc(mask_ready, 1)

            def maxima(B):
                back_step.begin(B)
                dve.wait_ge(mask_ready, B.count(1, 1))
                for t in T4:
                    for hd in H8:
                        dve.wait_ge(*scores.holds(f"s{t}_{hd}", B))
                        bank = scores.bank(f"s{t}_{hd}")
                        take_wait()
                        V.tensor_tensor_reduce(
                            out=junk[scores.place[f"s{t}_{hd}"][0]][0:ROWS, :], in0=bank[0:ROWS, 0:NP], in1=mask[par(B)][0:ROWS, t, MAXROWS:],
                            scale=1.0, scalar=-3e38, op0=ALU.add, op1=ALU.max,
                            accum_out=mx[0:ROWS, t, hd:hd + 1]).then_inc(scores.free_of(f"s{t}_{hd}"), 1)
                for sem_, n in scores.all_gone([f"s{NT - 1}_{hd}" for hd in H8], B):
                    dve.wait_ge(sem_, n)
                V.tensor_scalar(maxhl[0:ROWS, :, 0:HEADS], mx[0:ROWS, :, :], -1.0, None, ALU.mult).then_inc(vec_back_step, 1)
                dve.wait_ge(vec_back_step, back_step.next())
                V.scalar_tensor_tensor(out=maxhl[0:ROWS, :, HEADS:MAXROWS], in0=mx[0:ROWS, :, :], scalar=-1.0,
                                       in1=maxhl[0:ROWS, :, 0:HEADS], op0=ALU.mult, op1=ALU.subtract)\
                 .then_inc(maxhl_ready, 1)

            def norm(B, hd):
                dve.wait_ge(*rest.holds(f"pv{hd}", B))
                bank = rest.bank(f"pv{hd}")[0:ROWS, 0:NT * VW].rearrange("p (t w) -> p t w", t=NT)
                V.reciprocal(rden[0:ROWS, hd, :], bank[:, :, DH]).then_inc(vec_back_step, 1)
                dve.wait_ge(vec_back_step, back_step.next())
                V.tensor_tensor(o[0:ROWS, :, hd * DH:(hd + 1) * DH], bank[:, :, 0:DH],
                                             rden[0:ROWS, hd, :].unsqueeze(2).to_broadcast([ROWS, NT, DH]), ALU.mult).then_inc(rest.free_of(f"pv{hd}"), 1)

            def proj(B):
                dve.wait_ge(h_biased, B.count(1, 1))
                for t in T4:
                    dve.wait_ge(*rest.holds(f"proj{t}", B))
                    bank = rest.bank(f"proj{t}")
                    V.tensor_tensor(h2[0:ROWS, t, :], bank[0:ROWS, 0:E], h[par(B)][0:ROWS, t, :],
                                                 ALU.add).then_inc(rest.free_of(f"proj{t}"), 1)
                for sem_, n in rest.all_gone([f"proj{t}" for t in T4], B):
                    dve.wait_ge(sem_, n)
                layernorm(back_step, vec_back_step, B, h2, bn2, mv2, z2, var2_ready, rstd2, rstd2_ready, z2_ready)

            def ffn_in(B):
                for t in T4:
                    dve.wait_ge(*rest.holds(f"fx{t}", B))
                    bank = rest.bank(f"fx{t}")
                    V.tensor_tensor(fx[0:ROWS, t, :, 0:P],
                                                 bank[0:ROWS, :].rearrange("p (c k) -> p c k", c=PAIRS),
                                                 bfx_s[0:ROWS, :].rearrange("p (c k) -> p c k", c=PAIRS),
                                                 ALU.add).then_inc(rest.free_of(f"fx{t}"), 1)
                def wide(x, t):
                    return x[0:ROWS, t, :].unsqueeze(2).to_broadcast([ROWS, HEADS, SLICES])

                for t in T4:
                    dve.wait_ge(*rest.holds(f"logit{t}", B))
                    bank = rest.bank(f"logit{t}")
                    lt = logit[0:ROWS, t, :, :]
                    V.tensor_tensor(lt, bank[0:ROWS, :].rearrange("p (h g) -> p h g", h=HEADS),
                                                 blog_s[0:ROWS, :].rearrange("p (h g) -> p h g", h=HEADS),
                                                 ALU.add).then_inc(rest.free_of(f"logit{t}"), 1)
                    dve.wait_ge(*rest.gone(f"logit{t}", B))
                    V.tensor_reduce(lmax[0:ROWS, t, :], lt, AX, ALU.max).then_inc(vec_back_step, 1)
                    dve.wait_ge(vec_back_step, back_step.next())
                    V.tensor_tensor(lt, lt, wide(lmax, t), ALU.subtract).then_inc(logit_shifted, 1)
                for t in T4:
                    dve.wait_ge(logit_exped, B.count(NT, t + 1))
                    st = sw[0:ROWS, t, :, :]
                    V.tensor_reduce(lsum[0:ROWS, t, :], st, AX, ALU.add).then_inc(vec_back_step, 1)
                    dve.wait_ge(vec_back_step, back_step.next())
                    V.reciprocal(lsum[0:ROWS, t, :], lsum[0:ROWS, t, :]).then_inc(vec_back_step, 1)
                    dve.wait_ge(vec_back_step, back_step.next())
                    V.tensor_tensor(st, st, wide(lsum, t), ALU.mult).then_inc(sw_ready, 1)

            def tokens(B):
                for g in range(2):
                    dve.wait_ge(*rest.holds(f"token{g}", B))
                    bank = rest.bank(f"token{g}")[:, 0:2 * (P + 1)].rearrange("p (c k) -> p c k", c=2)
                    n = snorm[:, 2 * g:2 * g + 2]
                    V.tensor_scalar(n, bank[:, :, P], 1e-5, None, ALU.add).then_inc(vec_back_step, 1)
                    dve.wait_ge(vec_back_step, back_step.next())
                    V.reciprocal(n, n).then_inc(vec_back_step, 1)
                    dve.wait_ge(vec_back_step, back_step.next())
                    for j in range(2):
                        a = slice(j * DH, (j + 1) * DH)
                        last = V.tensor_tensor(token[a, 2 * g:2 * g + 2, a], bank[a, :, a],
                                               n[a, :].unsqueeze(2).to_broadcast([DH, 2, DH]), ALU.mult)
                    last.then_inc(rest.free_of(f"token{g}"), 1)

            def token_attn(B):
                dve.wait_ge(*rest.holds("s2", B))
                bank = rest.bank("s2")[:, 0:PAIRS * SLICES].rearrange("p (c k) -> p c k", c=PAIRS)
                V.tensor_reduce(amax[:, :], bank, AX, ALU.max).then_inc(vec_back_step, 1)
                dve.wait_ge(vec_back_step, back_step.next())
                V.tensor_tensor(ash[:, :, :], bank, amax[:, :].unsqueeze(2).to_broadcast([P, PAIRS, SLICES]),
                                             ALU.subtract).then_inc(rest.free_of("s2"), 1)
                dve.wait_ge(attn_exped, B.count(1, 1))
                V.tensor_reduce(asum[:, :], aexp[:, :, :], AX, ALU.add).then_inc(vec_back_step, 1)
                dve.wait_ge(vec_back_step, back_step.next())
                V.reciprocal(asum[:, :], asum[:, :]).then_inc(vec_back_step, 1)
                dve.wait_ge(vec_back_step, back_step.next())
                for j in range(2):
                    a = slice(j * DH, (j + 1) * DH)
                    last = V.tensor_tensor(attn[a, :, a], aexp[a, :, :],
                                           asum[a, :].unsqueeze(2).to_broadcast([DH, PAIRS, SLICES]), ALU.mult)
                last.then_inc(attn_ready, 1)

            def outputs(B):
                dve.wait_ge(h2_biased, B.count(1, 1))
                if B.back(1).exists():
                    dve.wait_ge(out_stored, B.back(1).count(32, 32))
                for t in T4:
                    dve.wait_ge(*rest.holds(f"out{t}", B))
                    bank = rest.bank(f"out{t}")
                    V.tensor_tensor(res[0:ROWS, t, :], bank[0:ROWS, 0:E], h2[0:ROWS, t, :], ALU.add).then_inc(rest.free_of(f"out{t}"), 1)

            def body(B, F):
                if B is not None:
                    maxima(B)
                if F is not None:
                    tok(F)
                if B is not None:
                    norm(B, 0)
                    norm(B, 1)
                if F is not None:
                    gram(F)
                    neighbours(F, 0)
                if B is not None:
                    norm(B, 2)
                if F is not None:
                    neighbours(F, 1)
                if B is not None:
                    norm(B, 3)
                if F is not None:
                    neighbours(F, 2)
                if B is not None:
                    norm(B, 4)
                if F is not None:
                    neighbours(F, 3)
                if B is not None:
                    norm(B, 5)
                    norm(B, 6)
                    norm(B, 7)
                    proj(B)
                    ffn_in(B)
                    tokens(B)
                    token_attn(B)
                    outputs(B)

            over_images(dve, body)

        @block.gpsimd
        def _(pool):
            G = nc.gpsimd
            root1_step = Steps(1)
            root2_step = Steps(1)
            pool.wait_ge(setup_vec, 1)
            pool.wait_ge(consts_in, 16 * len(consts))

            def root(steps, step_sem, img, var_sem, mv, ve, rstd, rstd_sem):
                steps.begin(img)
                pool.wait_ge(var_sem, img.count(1, 1))
                G.tensor_tensor(ve[0:ROWS, :], mv[0:ROWS, :, 1], eps_s[0:ROWS, :], ALU.add).then_inc(step_sem, 1)
                pool.wait_ge(step_sem, steps.next())
                G.tensor_tensor(rstd[0:ROWS, :], ve[0:ROWS, :], half_s[0:ROWS, :], ALU.pow).then_inc(rstd_sem, 1)

            def biased(img, x, bias, z_sem, done):
                pool.wait_ge(z_sem, img.count(1, 1))
                G.tensor_tensor(x[0:ROWS, :, :], x[0:ROWS, :, :],
                                bias[0:ROWS, :].unsqueeze(1).to_broadcast([ROWS, NT, E]), ALU.add)\
                 .then_inc(done, 1)

            def body(B, F):
                if F is not None:
                    root(root1_step, pool_root1_step, F, var1_ready, mv1, ve1, rstd1, rstd1_ready)
                    biased(F, h[par(F)], bout_s, z_ready, h_biased)
                if B is not None:
                    root(root2_step, pool_root2_step, B, var2_ready, mv2, ve2, rstd2, rstd2_ready)
                    biased(B, h2, bout2_s, z2_ready, h2_biased)

            over_images(pool, body)


def kernel(**inputs):
    import numpy as np
    import ml_dtypes
    import concourse.bacc as bacc
    from concourse.bass_utils import run_bass_kernel_spmd

    a = {k: np.asarray(w) for k, w in inputs.items()}

    def chunks(w):
        return w.reshape(-1, P, w.shape[1]).transpose(1, 0, 2)

    def rows(w):
        return np.broadcast_to(w.reshape(1, -1), (P, w.size))

    def twice(w):
        d = np.zeros((P, P), w.dtype)
        d[:DH, :DH] = w
        d[DH:, DH:] = w
        return d

    x = a["x"].reshape(BATCH, CHANNELS, GRID, PATCH, GRID, PATCH).transpose(0, 1, 3, 5, 2, 4)
    xt = np.zeros((BATCH, P, KT, NP), x.dtype)
    xt[..., :TOKENS] = x.reshape(BATCH, KT, P, TOKENS).transpose(0, 2, 1, 3)

    bf = ml_dtypes.bfloat16
    diag = np.zeros((P, NT, NP), np.float32)
    pick = np.zeros((P, HEADS, ROWS), np.float32)
    for t in range(NT):
        diag[np.arange(ROWS), t, t * ROWS + np.arange(ROWS)] = DIAG
        diag[:, t, TOKENS:] = DIAG
    for hd in range(HEADS):
        pick[hd, hd, :] = pick[HEADS + hd, hd, :] = 1
        pick[MAXROWS + np.arange(ROWS), hd, np.arange(ROWS)] = 1

    arrays = {
        "xt": xt,
        "wtok": chunks(a["L0_tok_W"].T),
        "btok": rows(a["L0_tok_b"]),
        "wqkv": chunks(a["L0_attn_Wqkv"]),
        "wout": chunks(a["L0_attn_Wout"]),
        "bout": rows(a["L0_attn_bout"]),
        "wfx": chunks(a["L0_ffn_W_fx"]),
        "bfx": rows(a["L0_ffn_b_fx"]),
        "wxT": chunks(a["L0_ffn_W_x"].T),
        "bx": a["L0_ffn_b_x"].reshape(PAIRS, P).T,
        "wslice": twice(a["L0_ffn_W_slice"]),
        "bslice": rows(np.tile(a["L0_ffn_b_slice"], HEADS)),
        "temp": rows(a["L0_ffn_temperature"]),
        "wq2": twice(a["L0_ffn_W_q"]),
        "wk2": twice(a["L0_ffn_W_k"]),
        "wv2": twice(a["L0_ffn_W_v"]),
        "wout2": chunks(a["L0_ffn_W_out"]),
        "bout2": rows(a["L0_ffn_b_out"]),
        "identf": np.eye(P, dtype=np.float32),
        "identb": np.eye(P, dtype=bf),
        "diag": diag.astype(bf),
        "pick": pick.astype(bf),
    }
    arrays = {k: np.ascontiguousarray(w) for k, w in arrays.items()}
    nc = bacc.Bacc("TRN2", target_bir_lowering=False, num_devices=1)
    args = {k: nc.dram_tensor(k, w.shape, mybir.dt.from_np(w.dtype), kind="ExternalInput").ap()
            for k, w in arrays.items()}
    out = nc.dram_tensor("out", (BATCH, TOKENS, E), mybir.dt.float32, kind="ExternalOutput").ap()
    build(nc, out=out, **args)
    r = run_bass_kernel_spmd(nc, [arrays], core_ids=[0])
    return r.results[0]["out"]
```

```python
import concourse.bass as bass
from concourse import mybir
from contextlib import ExitStack


BATCH, CHANNELS, SIDE, PATCH = 32, 3, 336, 16
GRID = SIDE // PATCH
TOKENS = GRID * GRID
E = 256
PATCH_K = CHANNELS * PATCH * PATCH
HEADS, DH, KNN = 8, 64, 32
SLICES = 64
INNER = HEADS * DH
P = 128
ROWS = 112
NT = 4
NP = ROWS * NT
LAST = TOKENS - (NT - 1) * ROWS
KT = PATCH_K // P
EC = E // P
PAIRS = HEADS // 2
MAXROWS = 2 * HEADS
SCALE = DH ** -0.5
EPS = 1e-5
OFF = -1e30
DIAG = -1e36
TAKEN = -3e38
TAKEN_BELOW = -2e38
assert MAXROWS + ROWS == P


class Image:

    def __init__(self, reg, off):
        self.reg, self.off = reg, off

    def count(self, per, k):
        c = self.off * per + k
        return c if self.reg is None else self.reg * (2 * per) + c

    def index(self):
        return self.off if self.reg is None else self.reg * 2 + self.off

    def back(self, n):
        return Image(self.reg, self.off - n)

    def exists(self):
        return self.reg is not None or self.off >= 0


class Ring:

    def __init__(self, banks, full, free, slots):
        self.banks, self.full, self.free = banks, full, free
        self.place, self.per = {}, [0] * len(banks)
        for n, name in enumerate(slots):
            b = n % len(banks)
            self.place[name] = (b, self.per[b])
            self.per[b] += 1

    def bank(self, name):
        return self.banks[self.place[name][0]]

    def full_of(self, name):
        return self.full[self.place[name][0]]

    def free_of(self, name):
        return self.free[self.place[name][0]]

    def emptied(self, name, img):
        b, k = self.place[name]
        return self.free[b], img.count(self.per[b], k)

    def holds(self, name, img):
        b, k = self.place[name]
        return self.full[b], img.count(self.per[b], k + 1)

    def gone(self, name, img):
        b, k = self.place[name]
        return self.free[b], img.count(self.per[b], k + 1)

    def all_gone(self, names, img):
        last = {}
        for name in sorted(names, key=lambda x: self.place[x][1]):
            last[self.place[name][0]] = name
        return [self.gone(name, img) for name in last.values()]


class Steps:

    def __init__(self, per):
        self.per, self.img, self.k = per, None, 0

    def begin(self, img):
        assert self.k in (0, self.per), (self.k, self.per)
        self.img, self.k = img, 0

    def next(self):
        self.k += 1
        return self.img.count(self.per, self.k)


def build(nc, xt, wtok, btok, wqkv, wout, bout, wfx, bfx, wxT, bx, wslice, bslice, temp,
          wqT2, wkT2, wvT2, wout2, bout2, identf, identb, diag, pick, out):
    fp32, bf16, fp16 = mybir.dt.float32, mybir.dt.bfloat16, mybir.dt.float16
    ALU, ACT, AX = mybir.AluOpType, mybir.ActivationFunctionType, mybir.AxisListType.X


    ctx = ExitStack()
    with ctx:
        def sb(name, shape, dt=fp32):
            return ctx.enter_context(nc.sbuf_tensor(name, shape, dt))

        def sem(name):
            return ctx.enter_context(nc.semaphore(name))

        consts = []

        def const(name, dram, dt=fp32):
            t = sb(name, list(dram.shape), dt)
            consts.append((t[:], dram))
            return t

        wtok_s = const("wtok_s", wtok)
        btok_s = const("btok_s", btok)
        wout_s = const("wout_s", wout)
        bout_s = const("bout_s", bout)
        bx_s = const("bx_s", bx)
        temp_s = const("temp_s", temp)
        bout2_s = const("bout2_s", bout2)
        identf_s = const("identf_s", identf)
        identb_s = const("identb_s", identb, bf16)
        diag_s = const("diag_s", diag, bf16)
        pick_s = const("pick_s", pick, bf16)
        ones_s = sb("ones_s", [P, P])
        half_s = sb("half_s", [P, NT])
        eps_s = sb("eps_s", [P, NT])
        wqkv_h, wqkv_l = sb("wqkv_h", [P, EC, 3 * INNER], fp16), sb("wqkv_l", [P, EC, 3 * INNER], fp16)
        wfx_h, wfx_l = sb("wfx_h", [P, EC, INNER], fp16), sb("wfx_l", [P, EC, INNER], fp16)
        wlog_h, wlog_l = sb("wlog_h", [P, EC, INNER], fp16), sb("wlog_l", [P, EC, INNER], fp16)
        bfx_rows, blog_rows = sb("bfx_rows", [P, INNER], fp16), sb("blog_rows", [P, INNER], fp16)
        ones_h = sb("ones_h", [P, ROWS], fp16)
        wqk_s = sb("wqk_s", [P, P])
        wvo_s = sb("wvo_s", [P, PAIRS, E])

        patches = sb("patches", [P, KT, NP])
        h = [sb(f"h{b}", [P, NT, E]) for b in range(2)]
        bn1 = sb("bn1", [P, NT, 6])
        mv1 = sb("mv1", [P, NT, 2])
        ve1 = sb("ve1", [P, NT])
        rstd1 = sb("rstd1", [P, NT])
        z = sb("z", [P, NT, E])
        zT_h, zT_l = sb("zT_h", [P, EC, NP], fp16), sb("zT_l", [P, EC, NP], fp16)
        early = sb("early", [P, 1024])
        zsq = early[:, 0:EC * NP].rearrange("p (c n) -> p c n", c=EC)
        x2 = sb("x2", [P, NP])
        scorebuf = sb("scorebuf", [P, NT * NP])
        score = scorebuf[:, :].rearrange("p (t n) -> p t n", t=NT)
        top8 = sb("top8", [P, NT, 8])
        mask = sb("mask", [P, NT, MAXROWS + NP], bf16)
        maskmax = sb("maskmax", [P, NT, NP], bf16)
        parts = {x: [sb(f"{x}_{y}", [P, PAIRS, NP], fp16) for y in "hl"] for x in "qk"}
        k_hl = sb("k_hl", [P, HEADS, NP], fp16)
        q_hl = sb("q_hl", [P, HEADS, NP], fp16)
        q_lh = sb("q_lh", [P, HEADS, NP], fp16)
        v1 = sb("v1", [P, NT, PAIRS, 2, P], fp16)
        v_l = sb("v_l", [P, NT, HEADS, DH], fp16)

        junk = [sb(f"junk{b}", [P, NP], bf16) for b in range(3)]
        mx = sb("mx", [P, NT, HEADS])
        maxhl = sb("maxhl", [P, NT, MAXROWS], bf16)
        heads = [sb(f"heads{b}", [P, NT * INNER]) for b in range(2)]
        probs = [x[:, 0:NT * NP].rearrange("p (t n) -> p t n", t=NT) for x in heads]
        probs_h = [sb(f"probs_h{b}", [P, NT, NP], fp16) for b in range(2)]
        probs_l = [sb(f"probs_l{b}", [P, NT, NP], fp16) for b in range(2)]
        rden = sb("rden", [P, 2, NP])
        oT = sb("oT", [P, PAIRS, NP])
        h2 = sb("h2", [P, NT, E])
        bn2 = sb("bn2", [P, NT, 6])
        mv2 = sb("mv2", [P, NT, 2])
        ve2 = sb("ve2", [P, NT])
        rstd2 = sb("rstd2", [P, NT])
        z2 = z
        z2T_h, z2T_l = [early[:, n * NP:(n + 1) * NP].bitcast(fp16).rearrange("p (c n) -> p c n", c=EC) for n in range(2)]
        fx = sb("fx", [P, NT, PAIRS, P + 1])
        logit, sw = [x[:, :].rearrange("p (t h g) -> p t h g", t=NT, h=HEADS) for x in heads]
        lmax = sb("lmax", [P, NT, HEADS])
        lsum = sb("lsum", [P, NT, HEADS])
        swT = oT
        snorm = sb("snorm", [P, PAIRS])
        token = sb("token", [P, PAIRS, P])
        late = [x[:, :, :].rearrange("p a b -> p (a b)").bitcast(fp32) for x in (*probs_h, *probs_l)]
        tokenT, tokenQ, attnT = [late[n][:, 0:PAIRS * P].rearrange("p (c k) -> p c k", c=PAIRS) for n in range(3)]
        tokenC = late[0][:, PAIRS * P:PAIRS * (P + SLICES)].rearrange("p (c k) -> p c k", c=PAIRS)
        ash, aexp = [late[3][:, n * 256:(n + 1) * 256].rearrange("p (c k) -> p c k", c=PAIRS) for n in range(2)]
        amax = sb("amax", [P, PAIRS])
        asum = sb("asum", [P, PAIRS])
        attn = sb("attn", [P, PAIRS, P])
        u = early[:, :].rearrange("p (c e) -> p c e", c=PAIRS)
        mix = scorebuf[:, 0:PAIRS * E].rearrange("p (c e) -> p c e", c=PAIRS)
        res = sb("res", [P, NT, E])

        wqk_f = heads[0][:, :].rearrange("p (c n) -> p c n", c=EC)
        wv_f, wfx_f = [heads[1][:, n * 1024:(n + 1) * 1024].rearrange("p (c n) -> p c n", c=EC) for n in range(2)]
        wxT_s = res[:, :, :]
        bslice_s = z[:, 0:2, :].rearrange("p a b -> p (a b)")
        bxrep = early[:, 0:PAIRS * P].rearrange("p (c k) -> p c k", c=PAIRS)
        wout2_s = h[0][:, :, :]
        bfx_s, blog_s = [rden[:, :, :].rearrange("p a b -> p (a b)")[:, 0:INNER], oT[:, 0:2, :].rearrange("p a b -> p (a b)")[:, 0:INNER]]
        wslice_s, wqT2_s, wkT2_s, wvT2_s = [scorebuf[:, n * P:(n + 1) * P] for n in range(4)]
        wlog_f = h[1][:, :, :].rearrange("p a b -> p (a b)").rearrange("p (c n) -> p c n", c=EC)
        consts += [(wqk_f, wqkv[:, :, 0:2 * INNER]), (wv_f, wqkv[:, :, 2 * INNER:]), (wfx_f, wfx), (wxT_s, wxT),
                   (bslice_s, bslice), (bfx_s, bfx), (wout2_s, wout2), (wslice_s, wslice), (wqT2_s, wqT2), (wkT2_s, wkT2),
                   (wvT2_s, wvT2)]

        def ring(name, n, slots):
            banks = [ctx.enter_context(nc.psum_tensor(f"{name}{b}", [P, 512], fp32)) for b in range(n)]
            return Ring(banks, [sem(f"{name}{b}_full") for b in range(n)],
                        [sem(f"{name}{b}_free") for b in range(n)], slots)

        T4, C4, H8 = range(NT), range(PAIRS), range(HEADS)
        front = ring("front", 2, [f"tok{t}" for t in T4] + ["zT0", "zT1", "x2"] + [f"gram{t}" for t in T4]
                     + [f"q{c}" for c in C4] + [f"k{c}" for c in C4] + [f"v{t}" for t in T4]
                     + [f"maskT{t}" for t in T4])
        scores = ring("scores", 3, [f"s{t}_{hd}" for t in T4 for hd in H8]
                      + [f"sT{hd}_{t}" for hd in H8 for t in T4])
        rest = ring("rest", 3, ["maxT"] + [f"pv{hd}" for hd in H8]
                    + [f"proj{t}" for t in T4] + ["z2T0", "z2T1"] + [f"logit{t}" for t in T4]
                    + [f"fx{t}" for t in T4] + [f"swT{c}" for c in C4] + ["token0", "token1", "tokenT",
                    "tokenQ", "s2", "u0", "u1", "attnT", "mix0", "mix1"]
                    + [f"out{t}" for t in T4])

        consts_in = sem("consts_in")
        setup_vec = sem("setup_vec")
        setup_chain = sem("setup_chain")
        setup_pe = sem("setup_pe")
        setup_act = sem("setup_act")
        patches_in = sem("patches_in")
        q_stacked = sem("q_stacked")
        k_stacked = sem("k_stacked")
        out_stored = sem("out_stored")
        var1_ready = sem("var1_ready")
        var2_ready = sem("var2_ready")
        rstd1_ready = sem("rstd1_ready")
        rstd2_ready = sem("rstd2_ready")
        z_ready = sem("z_ready")
        z2_ready = sem("z2_ready")
        zT_high = sem("zT_high")
        z2T_high = sem("z2T_high")
        qk_high = sem("qk_high")
        v_high = sem("v_high")
        h_biased = sem("h_biased")
        h2_biased = sem("h2_biased")
        mask_ready = sem("mask_ready")
        maxhl_ready = sem("maxhl_ready")
        probs_split = sem("probs_split")
        pair_normed = sem("pair_normed")
        probs_ready = sem("probs_ready")
        logit_exped = sem("logit_exped")
        sw_ready = sem("sw_ready")
        attn_exped = sem("attn_exped")
        tokenT_whole = sem("tokenT_whole")
        attn_ready = sem("attn_ready")
        vec_front_step = sem("vec_front_step")
        vec_back_step = sem("vec_back_step")
        pool_root1_step = sem("pool_root1_step")
        pool_root2_step = sem("pool_root2_step")

        block = ctx.enter_context(nc.Block())

        def over_images(eng, back_and_front):
            back_and_front(None, Image(None, 0))
            back_and_front(Image(None, 0), Image(None, 1))
            with eng.Fori(0, BATCH // 2 - 1) as i:
                back_and_front(Image(i, 1), Image(i, 2))
                back_and_front(Image(i, 2), Image(i, 3))
            back_and_front(Image(None, BATCH - 1), None)

        EARLY = 16
        TAIL = [range(n, min(n + 3, EARLY)) for n in range(0, 18, 3)]

        def par(img):
            return img.off % 2

        @block.sync
        def _(sp):
            def take_wait():
                sp.nop(nofuse=True)

            for t, dram in consts:
                sp.dma_start(t, dram).then_inc(consts_in, 16)

            def load(F):
                if F.back(1).exists():
                    sp.wait_ge(*front.holds("tok3", F.back(1)))
                    take_wait()
                sp.dma_start(patches[:], xt[F.index()]).then_inc(patches_in, 16)

            def stack(x, done, F, high_over_low):
                lo, hi = slice(0, DH), slice(DH, P)
                sp.wait_ge(*front.gone(f"{x}{PAIRS - 2}", F))
                take_wait()
                sp.wait_ge(*front.gone(f"{x}{PAIRS - 1}", F))
                take_wait()
                for part, src in enumerate(parts[x]):
                    for dst, first in high_over_low:
                        rows = lo if part == first else hi
                        sp.dma_start(dst[rows, 0:HEADS:2, :], src[lo, :, :]).then_inc(done, 16)
                        sp.dma_start(dst[rows, 1:HEADS:2, :], src[hi, :, :]).then_inc(done, 16)

            def store(B):
                for t in range(1, NT):
                    sp.wait_ge(*rest.gone(f"out{t}", B))
                    take_wait()
                n = B.index()
                sp.dma_start(out[n, 0:3 * ROWS, :].rearrange("(t p) e -> p t e", p=ROWS),
                             res[0:ROWS, 0:3, :]).then_inc(out_stored, 16)
                sp.dma_start(out[n, 3 * ROWS:TOKENS, :], res[0:LAST, 3, :]).then_inc(out_stored, 16)

            def body(B, F):
                if F is not None:
                    load(F)
                if B is not None and B.back(1).exists():
                    store(B.back(1))
                if F is not None:
                    stack("q", q_stacked, F, [(q_hl, 0), (q_lh, 1)])
                    stack("k", k_stacked, F, [(k_hl, 0)])

            over_images(sp, body)
            store(Image(None, BATCH - 1))
            sp.wait_ge(out_stored, 32 * BATCH)

        @block.tensor
        def _(pe):
            mm = nc.tensor.matmul
            pe.wait_ge(consts_in, 16 * len(consts))
            pe.wait_ge(setup_vec, 2)
            for c in range(EC):
                for p in C4:
                    last = mm(scores.banks[c][:, p * P:(p + 1) * P], wxT_s[:, p, c * P:(c + 1) * P],
                              wslice_s, start=True, stop=True)
            for p in C4:
                last = mm(scores.banks[2][:, p * P:(p + 1) * P], bxrep[:, p, :], wslice_s,
                          start=True, stop=True)
            mm(front.banks[0][:, 0:P], wqT2_s, wkT2_s, start=True, stop=True)
            for p in C4:
                last = mm(rest.banks[p // 2][:, (p % 2) * E:(p % 2 + 1) * E], wvT2_s, wout2_s[:, p, :],
                          start=True, stop=True)
            last.then_inc(setup_pe, 1)
            pe.wait_ge(setup_vec, 3)
            pe.wait_ge(setup_act, 1)

            def split_product(out_, lhs, rhs, first=True, last=True):
                mm(out_, lhs[0], rhs[0], start=first, stop=False)
                mm(out_, lhs[0], rhs[1], start=False, stop=False)
                return mm(out_, lhs[1], rhs[0], start=False, stop=last)

            def tok(F, steps):
                for t, k in [divmod(n, KT) for n in steps]:
                    if (t, k) == (0, 0):
                        pe.wait_ge(patches_in, F.count(16, 16))
                    if k == 0:
                        pe.wait_ge(*front.emptied(f"tok{t}", F))
                    last = mm(front.bank(f"tok{t}")[0:ROWS, 0:E], patches[:, k, t * ROWS:(t + 1) * ROWS],
                              wtok_s[:, k, :], start=(k == 0), stop=(k == KT - 1))
                    if k == KT - 1:
                        last.then_inc(front.full_of(f"tok{t}"), 1)

            def transposes(ring_, names, img, src):
                for c, name in enumerate(names):
                    pe.wait_ge(*ring_.emptied(name, img))
                    bank = ring_.bank(name)
                    for t in T4:
                        last = nc.tensor.transpose(bank[:, t * ROWS:(t + 1) * ROWS],
                                                   src[0:ROWS, t, c * P:(c + 1) * P], identf_s[0:ROWS, 0:ROWS])
                    last.then_inc(ring_.full_of(name), 1)

            def ztr(F):
                pe.wait_ge(z_ready, F.count(1, 1))
                transposes(front, ["zT0", "zT1"], F, z)

            def gram(F):
                for sem_, n in front.all_gone(["zT0", "zT1"], F):
                    pe.wait_ge(sem_, n)
                pe.wait_ge(*front.emptied("x2", F))
                bank = front.bank("x2")
                for c in range(EC):
                    last = mm(bank[0:ROWS, 0:NP], ones_s[:, 0:ROWS], zsq[:, c, :], start=(c == 0), stop=(c == 1))
                last.then_inc(front.full_of("x2"), 1)
                for t in T4:
                    pe.wait_ge(*front.emptied(f"gram{t}", F))
                    bank = front.bank(f"gram{t}")
                    rows = slice(t * ROWS, (t + 1) * ROWS)
                    for c in range(EC):
                        split_product(bank[0:ROWS, 0:NP], (zT_h[:, c, rows], zT_l[:, c, rows]),
                                      (zT_h[:, c, :], zT_l[:, c, :]), first=(c == 0), last=False)
                    last = mm(bank[0:ROWS, 0:NP], identb_s[0:ROWS, 0:ROWS], diag_s[0:ROWS, t, :],
                              start=False, stop=True)
                    last.then_inc(front.full_of(f"gram{t}"), 1)

            def qk(F, which):
                base = {"q": 0, "k": INNER}[which]
                for p in C4:
                    pe.wait_ge(*front.emptied(f"{which}{p}", F))
                    bank = front.bank(f"{which}{p}")
                    cols = slice(base + p * P, base + (p + 1) * P)
                    for c in range(EC):
                        last = split_product(bank[:, 0:NP], (wqkv_h[:, c, cols], wqkv_l[:, c, cols]),
                                             (zT_h[:, c, :], zT_l[:, c, :]), first=(c == 0), last=(c == 1))
                    last.then_inc(front.full_of(f"{which}{p}"), 1)

            def vals(F, ts):
                for t in ts:
                    pe.wait_ge(*front.emptied(f"v{t}", F))
                    bank = front.bank(f"v{t}")
                    rows = slice(t * ROWS, (t + 1) * ROWS)
                    for c in range(EC):
                        last = split_product(bank[0:ROWS, :], (zT_h[:, c, rows], zT_l[:, c, rows]),
                                             (wqkv_h[:, c, 2 * INNER:], wqkv_l[:, c, 2 * INNER:]),
                                             first=(c == 0), last=(c == 1))
                    last.then_inc(front.full_of(f"v{t}"), 1)

            def mask_tr(F, ts):
                pe.wait_ge(mask_ready, F.count(1, 1))
                for mt in ts:
                    pe.wait_ge(*front.emptied(f"maskT{mt}", F))
                    bank = front.bank(f"maskT{mt}").bitcast(bf16)
                    for t in T4:
                        last = nc.tensor.transpose(bank[:, t * ROWS:(t + 1) * ROWS],
                                                   mask[0:ROWS, t, mt * ROWS:mt * ROWS + P],
                                                   identb_s[0:ROWS, 0:ROWS])
                    last.then_inc(front.full_of(f"maskT{mt}"), 1)

            def score_rows(B, tiles):
                for t, hd in [divmod(n, HEADS) for n in tiles]:
                    if (t, hd) == (0, 0):
                        pe.wait_ge(q_stacked, B.count(128, 128))
                        pe.wait_ge(k_stacked, B.count(64, 64))
                    pe.wait_ge(*scores.emptied(f"s{t}_{hd}", B))
                    bank = scores.bank(f"s{t}_{hd}")
                    mm(bank[0:ROWS, 0:NP], q_hl[:, hd, t * ROWS:(t + 1) * ROWS], k_hl[:, hd, :],
                       start=True, stop=True).then_inc(scores.full_of(f"s{t}_{hd}"), 1)

            def max_tr(B):
                pe.wait_ge(maxhl_ready, B.count(1, 1))
                pe.wait_ge(*rest.emptied("maxT", B))
                bank = rest.bank("maxT").bitcast(bf16)
                for t in T4:
                    last = nc.tensor.transpose(bank[0:MAXROWS, t * ROWS:(t + 1) * ROWS],
                                               maxhl[0:ROWS, t, :], identb_s[0:ROWS, 0:ROWS])
                last.then_inc(rest.full_of("maxT"), 1)

            def score_cols(B, hd):
                if hd == 0:
                    for sem_, n in front.all_gone([f"maskT{t}" for t in T4], B):
                        pe.wait_ge(sem_, n)
                    pe.wait_ge(*rest.gone("maxT", B))
                for t in T4:
                    pe.wait_ge(*scores.emptied(f"sT{hd}_{t}", B))
                    bank = scores.bank(f"sT{hd}_{t}")
                    k_ = k_hl[:, hd, t * ROWS:(t + 1) * ROWS]
                    mm(bank[0:ROWS, 0:NP], k_, q_hl[:, hd, :], start=True, stop=False)
                    mm(bank[0:ROWS, 0:NP], k_, q_lh[:, hd, :], start=False, stop=False)
                    last = mm(bank[0:ROWS, 0:NP], pick_s[:, hd, :], maskmax[:, t, :], start=False, stop=True)
                    last.then_inc(scores.full_of(f"sT{hd}_{t}"), 1)

            def pv(B, hd):
                if hd == 0:
                    for sem_, n in front.all_gone([f"v{t}" for t in T4], B):
                        pe.wait_ge(sem_, n)
                pe.wait_ge(*rest.emptied(f"pv{hd}", B))
                bank = rest.bank(f"pv{hd}")
                b, own = hd % 2, slice((hd % 2) * DH, (hd % 2 + 1) * DH)
                for sem_, n in scores.all_gone([f"sT{hd}_{t}" for t in T4], B):
                    pe.wait_ge(sem_, n)
                for m in T4:
                    mm(bank[:, 0:NP], v1[0:ROWS, m, hd // 2, hd % 2, :], probs_h[b][0:ROWS, m, :],
                       start=(m == 0), stop=False)
                for m in T4:
                    mm(bank[own, 0:NP], v_l[0:ROWS, m, hd, :], probs_h[b][0:ROWS, m, :], start=False, stop=False)
                for m in T4:
                    pe.wait_ge(probs_ready, B.count(HEADS * NT, hd * NT + m + 1))
                    last = mm(bank[:, 0:NP], v1[0:ROWS, m, hd // 2, hd % 2, :], probs_l[b][0:ROWS, m, :],
                              start=False, stop=(m == NT - 1))
                last.then_inc(rest.full_of(f"pv{hd}"), 1)

            def rows_product(B, names, srcT, w, n):
                chunks = srcT.shape[1]
                for t in T4:
                    pe.wait_ge(*rest.emptied(names[t], B))
                    bank = rest.bank(names[t])
                    for c in range(chunks):
                        last = mm(bank[0:ROWS, 0:n], srcT[:, c, t * ROWS:(t + 1) * ROWS], w[:, c, :],
                                  start=(c == 0), stop=(c == chunks - 1))
                    last.then_inc(rest.full_of(names[t]), 1)

            def proj(B):
                pe.wait_ge(pair_normed, B.count(PAIRS, PAIRS))
                rows_product(B, [f"proj{t}" for t in T4], oT, wout_s, E)

            def ffn_transpose(B):
                pe.wait_ge(z2_ready, B.count(1, 1))
                transposes(rest, ["z2T0", "z2T1"], B, z2)

            def ffn_in(B, which, w_h, w_l, bias_rows):
                if which == "logit":
                    for sem_, n in rest.all_gone(["z2T0", "z2T1"], B):
                        pe.wait_ge(sem_, n)
                for t in T4:
                    pe.wait_ge(*rest.emptied(f"{which}{t}", B))
                    bank = rest.bank(f"{which}{t}")
                    rows = slice(t * ROWS, (t + 1) * ROWS)
                    for c in range(EC):
                        split_product(bank[0:ROWS, :], (z2T_h[:, c, rows], z2T_l[:, c, rows]),
                                      (w_h[:, c, :], w_l[:, c, :]), first=(c == 0), last=False)
                    last = mm(bank[0:ROWS, :], ones_h[:], bias_rows[:], start=False, stop=True)
                    last.then_inc(rest.full_of(f"{which}{t}"), 1)

            def sw_tr(B):
                pe.wait_ge(sw_ready, B.count(NT, NT))
                for c in C4:
                    pe.wait_ge(*rest.emptied(f"swT{c}", B))
                    bank = rest.bank(f"swT{c}")
                    for t in T4:
                        last = nc.tensor.transpose(bank[:, t * ROWS:(t + 1) * ROWS],
                                                   sw[0:ROWS, t, 2 * c:2 * c + 2, :], identf_s[0:ROWS, 0:ROWS])
                    last.then_inc(rest.full_of(f"swT{c}"), 1)

            def tokens(B):
                for sem_, n in rest.all_gone(["swT1", *[f"fx{t}" for t in T4]], B):
                    pe.wait_ge(sem_, n)
                for g in range(2):
                    pe.wait_ge(*rest.emptied(f"token{g}", B))
                    bank = rest.bank(f"token{g}")
                    for j in range(2):
                        p = 2 * g + j
                        for t in T4:
                            n = ROWS if t < NT - 1 else LAST
                            last = mm(bank[:, j * (P + 1):(j + 1) * (P + 1)], sw[0:n, t, 2 * p:2 * p + 2, :],
                                      fx[0:n, t, p, :], start=(t == 0), stop=(t == NT - 1))
                    last.then_inc(rest.full_of(f"token{g}"), 1)

            def square_tr(B, src, name):
                pe.wait_ge(*rest.emptied(name, B))
                bank = rest.bank(name)
                for p in C4:
                    last = nc.tensor.transpose(bank[:, p * P:(p + 1) * P], src[:, p, :], identf_s[:])
                last.then_inc(rest.full_of(name), 1)

            def token_tr(B):
                for sem_, n in rest.all_gone(["token0", "token1"], B):
                    pe.wait_ge(sem_, n)
                square_tr(B, token, "tokenT")

            def token_q(B):
                pe.wait_ge(tokenT_whole, B.count(1, 1))
                pe.wait_ge(*rest.emptied("tokenQ", B))
                mm(rest.bank("tokenQ")[:, :], wqk_s[:], tokenT[:, :, :], start=True, stop=True)\
                    .then_inc(rest.full_of("tokenQ"), 1)

            def token_scores(B):
                pe.wait_ge(*rest.gone("tokenT", B))
                pe.wait_ge(*rest.gone("tokenQ", B))
                pe.wait_ge(*rest.emptied("s2", B))
                bank = rest.bank("s2")
                for p in C4:
                    last = mm(bank[:, p * SLICES:(p + 1) * SLICES], tokenQ[:, p, :], tokenC[:, p, :],
                              start=True, stop=True)
                last.then_inc(rest.full_of("s2"), 1)

            def paired(B, names, lhs, rhs):
                for g in range(2):
                    pe.wait_ge(*rest.emptied(names[g], B))
                    bank = rest.bank(names[g])
                    for j in range(2):
                        p = 2 * g + j
                        last = mm(bank[:, j * E:(j + 1) * E], lhs[:, p, :], rhs[:, p, :], start=True, stop=True)
                    last.then_inc(rest.full_of(names[g]), 1)

            def body(B, F):
                if B is not None and F is not None:
                    for n in range(EARLY, NT * HEADS):
                        score_rows(B, [n])
                        tok(F, range(n - EARLY, n - EARLY + 1))
                    tok(F, range(NT * HEADS - EARLY, NT * KT))
                elif F is not None:
                    tok(F, range(NT * KT))
                else:
                    score_rows(B, range(EARLY, NT * HEADS))
                if B is not None:
                    max_tr(B)
                    score_cols(B, 0)
                    score_cols(B, 1)
                    pv(B, 0)
                if F is not None:
                    ztr(F)
                if B is not None:
                    score_cols(B, 2)
                    pv(B, 1)
                if F is not None:
                    gram(F)
                if B is not None:
                    for hd in range(3, HEADS):
                        score_cols(B, hd)
                        pv(B, hd - 1)
                    pv(B, HEADS - 1)
                if F is not None:
                    qk(F, "q")
                if B is not None:
                    proj(B)
                if F is not None:
                    qk(F, "k")
                if B is not None:
                    ffn_transpose(B)
                if F is not None:
                    vals(F, [0, 1])
                if B is not None:
                    ffn_in(B, "logit", wlog_h, wlog_l, blog_rows)
                    ffn_in(B, "fx", wfx_h, wfx_l, bfx_rows)
                if F is not None:
                    vals(F, [2, 3])
                    mask_tr(F, T4)
                if B is not None:
                    sw_tr(B)
                    tokens(B)
                if F is not None:
                    score_rows(F, TAIL[0])
                if B is not None:
                    token_tr(B)
                if F is not None:
                    score_rows(F, TAIL[1])
                if B is not None:
                    token_q(B)
                if F is not None:
                    score_rows(F, TAIL[2])
                if B is not None:
                    token_scores(B)
                    paired(B, ["u0", "u1"], tokenT, wvo_s)
                if F is not None:
                    score_rows(F, TAIL[3])
                if B is not None:
                    pe.wait_ge(attn_ready, B.count(1, 1))
                    square_tr(B, attn, "attnT")
                if F is not None:
                    score_rows(F, TAIL[4])
                if B is not None:
                    for sem_, n in rest.all_gone(["attnT", "u0", "u1"], B):
                        pe.wait_ge(sem_, n)
                    paired(B, ["mix0", "mix1"], attnT, u)
                if F is not None:
                    score_rows(F, TAIL[5])
                if B is not None:
                    for sem_, n in rest.all_gone(["attnT", "mix0", "mix1"], B):
                        pe.wait_ge(sem_, n)
                    rows_product(B, [f"out{t}" for t in T4], swT, mix, E)

            over_images(pe, body)

        @block.scalar
        def _(act):
            A = nc.scalar.activation

            act.wait_ge(consts_in, 16 * len(consts))
            A(wqkv_h[:, :, 0:2 * INNER], wqk_f, ACT.Copy)
            A(wqkv_h[:, :, 2 * INNER:], wv_f, ACT.Copy)
            A(wfx_h[:], wfx_f, ACT.Copy).then_inc(setup_act, 1)

            def copy(ring_, name, img, dst, width=None, src=None):
                act.wait_ge(*ring_.holds(name, img))
                bank = ring_.bank(name)
                A(dst, bank[:, 0:width] if src is None else src(bank), ACT.Copy).then_inc(ring_.free_of(name), 1)

            def front_transposed(F):
                for c in range(EC):
                    act.wait_ge(*front.holds(f"zT{c}", F))
                    bank = front.bank(f"zT{c}")
                    A(zsq[:, c, :], bank[:, 0:NP], ACT.Square)
                    A(zT_h[:, c, :], bank[:, 0:NP], ACT.Copy).then_inc(zT_high, 1)

            def norms(F):
                act.wait_ge(*front.holds("x2", F))
                if F.back(1).exists():
                    act.wait_ge(*front.gone("gram3", F.back(1)))
                A(x2[0:ROWS, :], front.bank("x2")[0:ROWS, 0:NP], ACT.Copy).then_inc(front.free_of("x2"), 1)

            def qk(F, which):
                for p in C4:
                    act.wait_ge(*front.holds(f"{which}{p}", F))
                    A(parts[which][0][:, p, :], front.bank(f"{which}{p}")[:, 0:NP], ACT.Copy).then_inc(qk_high, 1)

            def vals(F, ts):
                for t in ts:
                    act.wait_ge(*front.holds(f"v{t}", F))
                    bank = front.bank(f"v{t}")[0:ROWS, :].rearrange("p (c j d) -> p c j d", c=PAIRS, j=2)
                    A(v1[0:ROWS, t, :, 0, 0:DH], bank[:, :, 0, :], ACT.Copy)
                    A(v1[0:ROWS, t, :, 1, DH:P], bank[:, :, 1, :], ACT.Copy).then_inc(v_high, 1)

            def masks(F):
                for t in T4:
                    copy(front, f"maskT{t}", F, maskmax[:, t, :], src=lambda bank: bank.bitcast(bf16)[:, 0:NP])

            def maxima(B):
                act.wait_ge(*rest.holds("maxT", B))
                bank = rest.bank("maxT").bitcast(bf16)
                for t in T4:
                    last = A(maskmax[0:MAXROWS, t, :], bank[0:MAXROWS, 0:NP], ACT.Copy)
                last.then_inc(rest.free_of("maxT"), 1)

            def exps(B, hd):
                for t in T4:
                    act.wait_ge(*scores.holds(f"sT{hd}_{t}", B))
                    bank = scores.bank(f"sT{hd}_{t}")[0:ROWS, 0:NP]
                    A(probs[hd % 2][0:ROWS, t, :], bank, ACT.Exp, scale=SCALE).then_inc(probs_split, 1)
                    A(probs_h[hd % 2][0:ROWS, t, :], bank, ACT.Exp, scale=SCALE)\
                        .then_inc(scores.free_of(f"sT{hd}_{t}"), 1)

            def outputs_and_sums(B, hd):
                own, other = slice((hd % 2) * DH, (hd % 2 + 1) * DH), slice((1 - hd % 2) * DH, (2 - hd % 2) * DH)
                p = hd // 2
                if hd % 2 == 0 and p >= 2:
                    act.wait_ge(pair_normed, B.count(PAIRS, p - 1))
                act.wait_ge(*rest.holds(f"pv{hd}", B))
                bank = rest.bank(f"pv{hd}")
                A(oT[own, p, :], bank[own, 0:NP], ACT.Copy)
                last = A(rden[own, p % 2, :], bank[other, 0:NP], ACT.Copy)
                last.then_inc(rest.free_of(f"pv{hd}"), 1)

            def body(B, F):
                if B is not None:
                    maxima(B)
                    exps(B, 0)
                    exps(B, 1)
                if F is not None:
                    front_transposed(F)
                if B is not None:
                    exps(B, 2)
                    outputs_and_sums(B, 0)
                if F is not None:
                    norms(F)
                if B is not None:
                    for hd in range(3, HEADS):
                        exps(B, hd)
                        outputs_and_sums(B, hd - 2)
                    outputs_and_sums(B, HEADS - 2)
                    outputs_and_sums(B, HEADS - 1)
                if F is not None:
                    qk(F, "q")
                    qk(F, "k")
                if B is not None:
                    for c in range(EC):
                        act.wait_ge(*rest.holds(f"z2T{c}", B))
                        A(z2T_h[:, c, :], rest.bank(f"z2T{c}")[:, 0:NP], ACT.Copy).then_inc(z2T_high, 1)
                if F is not None:
                    vals(F, [0, 1])
                if B is not None:
                    for t in T4:
                        act.wait_ge(*rest.gone(f"logit{t}", B))
                        A(sw[0:ROWS, t, :, :], logit[0:ROWS, t, :, :], ACT.Exp).then_inc(logit_exped, 1)
                        copy(rest, f"fx{t}", B, fx[0:ROWS, t, :, 0:P],
                             src=lambda bank: bank[0:ROWS, :].rearrange("p (c k) -> p c k", c=PAIRS))
                if F is not None:
                    vals(F, [2, 3])
                    masks(F)
                if B is not None:
                    for c in C4:
                        copy(rest, f"swT{c}", B, swT[:, c, :], NP)
                    act.wait_ge(*rest.holds("tokenT", B))
                    bank = rest.bank("tokenT")[:, :].rearrange("p (c k) -> p c k", c=PAIRS)
                    A(tokenT[:, :, :], bank, ACT.Copy).then_inc(tokenT_whole, 1)
                    A(tokenC[0:DH, :, :], bank[0:DH, :, 0:SLICES], ACT.Copy)
                    A(tokenC[DH:P, :, :], bank[DH:P, :, SLICES:P], ACT.Copy).then_inc(rest.free_of("tokenT"), 1)
                    copy(rest, "tokenQ", B, tokenQ[:, :, :], 512)
                    act.wait_ge(*rest.gone("s2", B))
                    A(aexp[:, :, :], ash[:, :, :], ACT.Exp, scale=SCALE).then_inc(attn_exped, 1)
                    for g in range(2):
                        copy(rest, f"u{g}", B, u[:, 2 * g:2 * g + 2, :], 512)
                    copy(rest, "attnT", B, attnT[:, :, :], 512)
                    for g in range(2):
                        copy(rest, f"mix{g}", B, mix[:, 2 * g:2 * g + 2, :], 512)

            over_images(act, body)

        @block.vector
        def _(dve):
            V = nc.vector

            def take_wait():
                dve.nop(nofuse=True)

            back_step = Steps(1 + PAIRS + 1 + 3 * NT + 4 + 3)
            front_step = Steps(1 + 8 * NT)

            def low_part(dst, x, high):
                return V.tensor_tensor(dst, x, high, ALU.subtract)

            V.memset(ones_s[:], 1.0)
            V.memset(ones_h[:], 1.0)
            V.memset(bfx_rows[:], 0.0)
            V.memset(blog_rows[:], 0.0)
            V.memset(half_s[:], -0.5)
            V.memset(eps_s[:], EPS)
            V.memset(mask[:, :, 0:MAXROWS], 0.0)
            V.memset(v1[:], 1.0)
            V.memset(fx[:, :, :, P:P + 1], 1.0)
            V.memset(token[:], 0.0)
            V.memset(attn[:], 0.0).then_inc(setup_vec, 1)
            dve.wait_ge(consts_in, 16 * len(consts))
            V.tensor_scalar(temp_s[:], temp_s[:], 0.1, 5.0, ALU.max, ALU.min).then_inc(setup_chain, 1)
            V.tensor_copy(bxrep, bx_s[:, :].unsqueeze(2).to_broadcast([P, PAIRS, P])).then_inc(setup_vec, 1)
            dve.wait_ge(setup_chain, 1)
            V.reciprocal(temp_s[:], temp_s[:]).then_inc(setup_chain, 1)
            dve.wait_ge(setup_act, 1)
            low_part(wqkv_l[:, :, 0:2 * INNER], wqk_f, wqkv_h[:, :, 0:2 * INNER])
            low_part(wqkv_l[:, :, 2 * INNER:], wv_f, wqkv_h[:, :, 2 * INNER:])
            low_part(wfx_l[:], wfx_f, wfx_h[:])
            dve.wait_ge(setup_chain, 2)
            invt = temp_s[:, :].unsqueeze(2).to_broadcast([P, HEADS, SLICES])
            dve.wait_ge(setup_pe, 1)
            V.tensor_copy(wqk_s[:], front.banks[0][:, 0:P])
            for g in range(2):
                V.tensor_copy(wvo_s[:, 2 * g:2 * g + 2, :], rest.banks[g][:, :].rearrange("p (c e) -> p c e", c=2))
            V.tensor_tensor(blog_s, scores.banks[2][:, :], bslice_s, ALU.add)
            V.tensor_copy(bfx_rows[0:1, :], bfx_s[0:1, :])
            for c in range(EC):
                last = V.tensor_tensor(wlog_f[:, c, :].rearrange("p (h g) -> p h g", h=HEADS),
                                       scores.banks[c][:, :].rearrange("p (h g) -> p h g", h=HEADS), invt, ALU.mult)
            last.then_inc(setup_chain, 1)
            dve.wait_ge(setup_chain, 3)
            V.tensor_copy(wlog_h[:], wlog_f).then_inc(setup_chain, 1)
            V.tensor_tensor(blog_s.rearrange("p (h g) -> p h g", h=HEADS),
                            blog_s.rearrange("p (h g) -> p h g", h=HEADS), invt, ALU.mult).then_inc(setup_chain, 1)
            dve.wait_ge(setup_chain, 5)
            V.tensor_copy(blog_rows[0:1, :], blog_s[0:1, :]).then_inc(setup_chain, 1)
            low_part(wlog_l[:], wlog_f, wlog_h[:])
            low_part(bfx_rows[32:33, :], bfx_s[0:1, :], bfx_rows[0:1, :])
            dve.wait_ge(setup_chain, 6)
            low_part(blog_rows[32:33, :], blog_s[0:1, :], blog_rows[0:1, :]).then_inc(setup_vec, 1)
            dve.wait_ge(setup_vec, 3)

            def layernorm(steps, step_sem, img, src, bn, mv, dst, var_sem, rstd, rstd_sem, dst_sem):
                for t in T4:
                    last = V.bn_stats(bn[0:ROWS, t, :], src[0:ROWS, t, :])
                last.then_inc(step_sem, 1)
                dve.wait_ge(step_sem, steps.next())
                take_wait()
                for t in T4:
                    last = V.bn_aggr(mv[0:ROWS, t, :], bn[0:ROWS, t, :])
                last.then_inc(var_sem, 1)
                dve.wait_ge(rstd_sem, img.count(1, 1))
                for t in T4:
                    last = V.tensor_scalar(dst[0:ROWS, t, :], src[0:ROWS, t, :], mv[0:ROWS, t, 0:1],
                                           rstd[0:ROWS, t:t + 1], ALU.subtract, ALU.mult)
                last.then_inc(dst_sem, 1)

            def tok(F, ts):
                for t in ts:
                    dve.wait_ge(*front.holds(f"tok{t}", F))
                    V.tensor_tensor(h[par(F)][0:ROWS, t, :], front.bank(f"tok{t}")[0:ROWS, 0:E],
                                    btok_s[0:ROWS, :], ALU.add).then_inc(front.free_of(f"tok{t}"), 1)

            def tok_norm(F):
                front_step.begin(F)
                for sem_, n in front.all_gone([f"tok{t}" for t in T4], F):
                    dve.wait_ge(sem_, n)
                layernorm(front_step, vec_front_step, F, h[par(F)], bn1, mv1, z, var1_ready, rstd1, rstd1_ready,
                          z_ready)

            def low_transposed(ring_, name, high_sem, low, high, img):
                for c in range(EC):
                    dve.wait_ge(high_sem, img.count(EC, c + 1))
                    low_part(low[:, c, :], ring_.bank(f"{name}{c}")[:, 0:NP], high[:, c, :])\
                        .then_inc(ring_.free_of(f"{name}{c}"), 1)

            def gram(F):
                dve.wait_ge(*front.gone("x2", F))
                for t in T4:
                    dve.wait_ge(*front.holds(f"gram{t}", F))
                    V.scalar_tensor_tensor(out=score[0:ROWS, t, :], in0=front.bank(f"gram{t}")[0:ROWS, 0:NP],
                                           scalar=2.0, in1=x2[0:ROWS, :], op0=ALU.mult,
                                           op1=ALU.subtract).then_inc(front.free_of(f"gram{t}"), 1)

            def neighbours(F, t):
                dve.wait_ge(*front.gone(f"gram{t}", F))
                row = score[0:ROWS, t, :]
                for r in range(KNN // 8):
                    take_wait()
                    V.max(out=top8[0:ROWS, t, :], in_=row).then_inc(vec_front_step, 1)
                    dve.wait_ge(vec_front_step, front_step.next())
                    take_wait()
                    V.match_replace(out=row, in_to_replace=top8[0:ROWS, t, :], in_values=row,
                                    imm_value=TAKEN).then_inc(vec_front_step, 1)
                    dve.wait_ge(vec_front_step, front_step.next())
                last = V.tensor_scalar(mask[0:ROWS, t, MAXROWS:], row, TAKEN_BELOW, OFF, ALU.is_gt, ALU.mult)
                if t == NT - 1:
                    last.then_inc(mask_ready, 1)

            def low_qk(F, which):
                for p in C4:
                    dve.wait_ge(qk_high, F.count(2 * PAIRS, "qk".index(which) * PAIRS + p + 1))
                    low_part(parts[which][1][:, p, :], front.bank(f"{which}{p}")[:, 0:NP],
                             parts[which][0][:, p, :]).then_inc(front.free_of(f"{which}{p}"), 1)

            def low_vals(F, ts):
                for t in ts:
                    dve.wait_ge(v_high, F.count(NT, t + 1))
                    bank = front.bank(f"v{t}")[0:ROWS, :].rearrange("p (c j d) -> p c j d", c=PAIRS, j=2)
                    low = v_l[0:ROWS, t, :, :].rearrange("p (c j) d -> p c j d", j=2)
                    low_part(low[:, :, 0, :], bank[:, :, 0, :], v1[0:ROWS, t, :, 0, 0:DH])
                    low_part(low[:, :, 1, :], bank[:, :, 1, :], v1[0:ROWS, t, :, 1, DH:P])\
                        .then_inc(front.free_of(f"v{t}"), 1)

            def row_maxima(B, tiles):
                for t, hd in [divmod(n, HEADS) for n in tiles]:
                    name = f"s{t}_{hd}"
                    if (t, hd) == (0, 0):
                        dve.wait_ge(mask_ready, B.count(1, 1))
                    dve.wait_ge(*scores.holds(name, B))
                    take_wait()
                    V.tensor_tensor_reduce(
                        out=junk[scores.place[name][0]][0:ROWS, :], in0=scores.bank(name)[0:ROWS, 0:NP],
                        in1=mask[0:ROWS, t, MAXROWS:], scale=1.0, scalar=-3e38, op0=ALU.add, op1=ALU.max,
                        accum_out=mx[0:ROWS, t, hd:hd + 1]).then_inc(scores.free_of(name), 1)

            def maxima_parts(B):
                back_step.begin(B)
                for sem_, n in scores.all_gone([f"s{NT - 1}_{hd}" for hd in H8], B):
                    dve.wait_ge(sem_, n)
                V.tensor_scalar(maxhl[0:ROWS, :, 0:HEADS], mx[0:ROWS, :, :], -1.0, None, ALU.mult)\
                    .then_inc(vec_back_step, 1)
                dve.wait_ge(vec_back_step, back_step.next())
                V.scalar_tensor_tensor(out=maxhl[0:ROWS, :, HEADS:MAXROWS], in0=mx[0:ROWS, :, :], scalar=-1.0,
                                       in1=maxhl[0:ROWS, :, 0:HEADS], op0=ALU.mult, op1=ALU.subtract)\
                 .then_inc(maxhl_ready, 1)

            def norm(B, p):
                dve.wait_ge(*rest.gone(f"pv{2 * p}", B))
                dve.wait_ge(*rest.gone(f"pv{2 * p + 1}", B))
                V.reciprocal(rden[:, p % 2, :], rden[:, p % 2, :]).then_inc(vec_back_step, 1)
                dve.wait_ge(vec_back_step, back_step.next())
                V.tensor_tensor(oT[:, p, :], oT[:, p, :], rden[:, p % 2, :], ALU.mult).then_inc(pair_normed, 1)

            def proj(B):
                dve.wait_ge(h_biased, B.count(1, 1))
                for t in T4:
                    dve.wait_ge(*rest.holds(f"proj{t}", B))
                    V.tensor_tensor(h2[0:ROWS, t, :], rest.bank(f"proj{t}")[0:ROWS, 0:E], h[par(B)][0:ROWS, t, :],
                                    ALU.add).then_inc(rest.free_of(f"proj{t}"), 1)
                for sem_, n in rest.all_gone([f"proj{t}" for t in T4], B):
                    dve.wait_ge(sem_, n)
                layernorm(back_step, vec_back_step, B, h2, bn2, mv2, z2, var2_ready, rstd2, rstd2_ready, z2_ready)

            def wide(x, t):
                return x[0:ROWS, t, :].unsqueeze(2).to_broadcast([ROWS, HEADS, SLICES])

            def ffn_shift(B):
                for t in T4:
                    dve.wait_ge(*rest.holds(f"logit{t}", B))
                    bank = rest.bank(f"logit{t}")[0:ROWS, :].rearrange("p (h g) -> p h g", h=HEADS)
                    V.tensor_reduce(lmax[0:ROWS, t, :], bank, AX, ALU.max).then_inc(vec_back_step, 1)
                    dve.wait_ge(vec_back_step, back_step.next())
                    V.tensor_tensor(logit[0:ROWS, t, :, :], bank, wide(lmax, t), ALU.subtract)\
                        .then_inc(rest.free_of(f"logit{t}"), 1)

            def ffn_softmax(B):
                for t in T4:
                    st = sw[0:ROWS, t, :, :]
                    dve.wait_ge(logit_exped, B.count(NT, t + 1))
                    V.tensor_reduce(lsum[0:ROWS, t, :], st, AX, ALU.add).then_inc(vec_back_step, 1)
                    dve.wait_ge(vec_back_step, back_step.next())
                    V.reciprocal(lsum[0:ROWS, t, :], lsum[0:ROWS, t, :]).then_inc(vec_back_step, 1)
                    dve.wait_ge(vec_back_step, back_step.next())
                    V.tensor_tensor(st, st, wide(lsum, t), ALU.mult).then_inc(sw_ready, 1)

            def tokens(B):
                for g in range(2):
                    dve.wait_ge(*rest.holds(f"token{g}", B))
                    bank = rest.bank(f"token{g}")[:, 0:2 * (P + 1)].rearrange("p (c k) -> p c k", c=2)
                    n = snorm[:, 2 * g:2 * g + 2]
                    V.tensor_scalar(n, bank[:, :, P], 1e-5, None, ALU.add).then_inc(vec_back_step, 1)
                    dve.wait_ge(vec_back_step, back_step.next())
                    V.reciprocal(n, n).then_inc(vec_back_step, 1)
                    dve.wait_ge(vec_back_step, back_step.next())
                    for j in range(2):
                        a = slice(j * DH, (j + 1) * DH)
                        last = V.tensor_tensor(token[a, 2 * g:2 * g + 2, a], bank[a, :, a],
                                               n[a, :].unsqueeze(2).to_broadcast([DH, 2, DH]), ALU.mult)
                    last.then_inc(rest.free_of(f"token{g}"), 1)

            def token_shift(B):
                dve.wait_ge(*rest.holds("s2", B))
                bank = rest.bank("s2")[:, 0:PAIRS * SLICES].rearrange("p (c k) -> p c k", c=PAIRS)
                V.tensor_reduce(amax[:, :], bank, AX, ALU.max).then_inc(vec_back_step, 1)
                dve.wait_ge(vec_back_step, back_step.next())
                V.tensor_tensor(ash[:, :, :], bank, amax[:, :].unsqueeze(2).to_broadcast([P, PAIRS, SLICES]),
                                ALU.subtract).then_inc(rest.free_of("s2"), 1)

            def token_attn(B):
                dve.wait_ge(attn_exped, B.count(1, 1))
                V.tensor_reduce(asum[:, :], aexp[:, :, :], AX, ALU.add).then_inc(vec_back_step, 1)
                dve.wait_ge(vec_back_step, back_step.next())
                V.reciprocal(asum[:, :], asum[:, :]).then_inc(vec_back_step, 1)
                dve.wait_ge(vec_back_step, back_step.next())
                for j in range(2):
                    a = slice(j * DH, (j + 1) * DH)
                    last = V.tensor_tensor(attn[a, :, a], aexp[a, :, :],
                                           asum[a, :].unsqueeze(2).to_broadcast([DH, PAIRS, SLICES]), ALU.mult)
                last.then_inc(attn_ready, 1)

            def outputs(B):
                dve.wait_ge(h2_biased, B.count(1, 1))
                if B.back(1).exists():
                    dve.wait_ge(out_stored, B.back(1).count(32, 32))
                for t in T4:
                    dve.wait_ge(*rest.holds(f"out{t}", B))
                    V.tensor_tensor(res[0:ROWS, t, :], rest.bank(f"out{t}")[0:ROWS, 0:E], h2[0:ROWS, t, :],
                                    ALU.add).then_inc(rest.free_of(f"out{t}"), 1)

            def body(B, F):
                if B is not None:
                    for n in range(EARLY, NT * HEADS):
                        row_maxima(B, [n])
                        if F is not None and n == EARLY + KT:
                            tok(F, [0])
                        if F is not None and n == EARLY + 2 * KT:
                            tok(F, [1])
                    maxima_parts(B)
                if F is not None:
                    tok(F, T4 if B is None else T4[2:])
                    tok_norm(F)
                    low_transposed(front, "zT", zT_high, zT_l, zT_h, F)
                    gram(F)
                    neighbours(F, 0)
                if B is not None:
                    norm(B, 0)
                if F is not None:
                    neighbours(F, 1)
                if B is not None:
                    norm(B, 1)
                if F is not None:
                    neighbours(F, 2)
                if B is not None:
                    norm(B, 2)
                    norm(B, 3)
                if F is not None:
                    low_qk(F, "q")
                if B is not None:
                    proj(B)
                if F is not None:
                    low_qk(F, "k")
                if B is not None:
                    low_transposed(rest, "z2T", z2T_high, z2T_l, z2T_h, B)
                if F is not None:
                    low_vals(F, [0, 1])
                if B is not None:
                    ffn_shift(B)
                    ffn_softmax(B)
                if F is not None:
                    neighbours(F, 3)
                    low_vals(F, [2, 3])
                if B is not None:
                    tokens(B)
                if F is not None:
                    row_maxima(F, TAIL[0])
                    row_maxima(F, TAIL[1])
                    row_maxima(F, TAIL[2])
                if B is not None:
                    token_shift(B)
                if F is not None:
                    row_maxima(F, TAIL[3])
                if B is not None:
                    token_attn(B)
                if F is not None:
                    row_maxima(F, TAIL[4])
                    row_maxima(F, TAIL[5])
                if B is not None:
                    outputs(B)

            over_images(dve, body)

        @block.gpsimd
        def _(pool):
            G = nc.gpsimd
            root1_step = Steps(1)
            root2_step = Steps(1)
            pool.wait_ge(setup_vec, 1)
            pool.wait_ge(consts_in, 16 * len(consts))

            def low_probs(B, hd):
                for t in T4:
                    pool.wait_ge(probs_split, B.count(HEADS * NT, hd * NT + t + 1))
                    pool.wait_ge(*scores.gone(f"sT{hd}_{t}", B))
                    G.tensor_tensor(probs_l[hd % 2][0:ROWS, t, :], probs[hd % 2][0:ROWS, t, :],
                                    probs_h[hd % 2][0:ROWS, t, :], ALU.subtract).then_inc(probs_ready, 1)

            def root(steps, step_sem, img, var_sem, mv, ve, rstd, rstd_sem):
                steps.begin(img)
                pool.wait_ge(var_sem, img.count(1, 1))
                G.tensor_tensor(ve[0:ROWS, :], mv[0:ROWS, :, 1], eps_s[0:ROWS, :], ALU.add).then_inc(step_sem, 1)
                pool.wait_ge(step_sem, steps.next())
                G.tensor_tensor(rstd[0:ROWS, :], ve[0:ROWS, :], half_s[0:ROWS, :], ALU.pow).then_inc(rstd_sem, 1)

            def biased(img, x, bias, z_sem, done):
                pool.wait_ge(z_sem, img.count(1, 1))
                G.tensor_tensor(x[0:ROWS, :, :], x[0:ROWS, :, :],
                                bias[0:ROWS, :].unsqueeze(1).to_broadcast([ROWS, NT, E]), ALU.add)\
                 .then_inc(done, 1)

            def body(B, F):
                if F is not None:
                    root(root1_step, pool_root1_step, F, var1_ready, mv1, ve1, rstd1, rstd1_ready)
                if B is not None:
                    for hd in H8:
                        low_probs(B, hd)
                if F is not None:
                    biased(F, h[par(F)], bout_s, z_ready, h_biased)
                if B is not None:
                    root(root2_step, pool_root2_step, B, var2_ready, mv2, ve2, rstd2, rstd2_ready)
                    biased(B, h2, bout2_s, z2_ready, h2_biased)

            over_images(pool, body)


def kernel(**inputs):
    import numpy as np
    import ml_dtypes
    import concourse.bacc as bacc
    from concourse.bass_utils import run_bass_kernel_spmd

    a = {k: np.asarray(w) for k, w in inputs.items()}

    def chunks(w):
        return w.reshape(-1, P, w.shape[1]).transpose(1, 0, 2)

    def rows(w):
        return np.broadcast_to(w.reshape(1, -1), (P, w.size))

    def twice(w):
        d = np.zeros((P, P), w.dtype)
        d[:DH, :DH] = w
        d[DH:, DH:] = w
        return d

    x = a["x"].reshape(BATCH, CHANNELS, GRID, PATCH, GRID, PATCH).transpose(0, 1, 3, 5, 2, 4)
    xt = np.zeros((BATCH, P, KT, NP), x.dtype)
    xt[..., :TOKENS] = x.reshape(BATCH, KT, P, TOKENS).transpose(0, 2, 1, 3)

    bf = ml_dtypes.bfloat16
    diag = np.zeros((P, NT, NP), np.float32)
    pick = np.zeros((P, HEADS, ROWS), np.float32)
    for t in range(NT):
        diag[np.arange(ROWS), t, t * ROWS + np.arange(ROWS)] = DIAG
        diag[:, t, TOKENS:] = DIAG
    for hd in range(HEADS):
        pick[hd, hd, :] = pick[HEADS + hd, hd, :] = 1
        pick[MAXROWS + np.arange(ROWS), hd, np.arange(ROWS)] = 1

    arrays = {
        "xt": xt,
        "wtok": chunks(a["L0_tok_W"].T),
        "btok": rows(a["L0_tok_b"]),
        "wqkv": chunks(a["L0_attn_Wqkv"]),
        "wout": chunks(a["L0_attn_Wout"]),
        "bout": rows(a["L0_attn_bout"]),
        "wfx": chunks(a["L0_ffn_W_fx"]),
        "bfx": rows(a["L0_ffn_b_fx"]),
        "wxT": chunks(a["L0_ffn_W_x"].T),
        "bx": a["L0_ffn_b_x"].reshape(PAIRS, P).T,
        "wslice": twice(a["L0_ffn_W_slice"]),
        "bslice": rows(np.tile(a["L0_ffn_b_slice"], HEADS)),
        "temp": rows(a["L0_ffn_temperature"]),
        "wqT2": twice(a["L0_ffn_W_q"].T),
        "wkT2": twice(a["L0_ffn_W_k"].T),
        "wvT2": twice(a["L0_ffn_W_v"].T),
        "wout2": chunks(a["L0_ffn_W_out"]),
        "bout2": rows(a["L0_ffn_b_out"]),
        "identf": np.eye(P, dtype=np.float32),
        "identb": np.eye(P, dtype=bf),
        "diag": diag.astype(bf),
        "pick": pick.astype(bf),
    }
    arrays = {k: np.ascontiguousarray(w) for k, w in arrays.items()}
    nc = bacc.Bacc("TRN2", target_bir_lowering=False, num_devices=1)
    args = {k: nc.dram_tensor(k, w.shape, mybir.dt.from_np(w.dtype), kind="ExternalInput").ap()
            for k, w in arrays.items()}
    out = nc.dram_tensor("out", (BATCH, TOKENS, E), mybir.dt.float32, kind="ExternalOutput").ap()
    build(nc, out=out, **args)
    r = run_bass_kernel_spmd(nc, [arrays], core_ids=[0])
    return r.results[0]["out"]
```

```python
import concourse.bass as bass
from concourse import mybir
from contextlib import ExitStack


BATCH, CHANNELS, SIDE, PATCH = 32, 3, 336, 16
GRID = SIDE // PATCH
TOKENS = GRID * GRID
E = 256
PATCH_K = CHANNELS * PATCH * PATCH
HEADS, DH, KNN = 8, 64, 32
SLICES = 64
INNER = HEADS * DH
P = 128
ROWS = 112
NT = 4
NP = ROWS * NT
LAST = TOKENS - (NT - 1) * ROWS
KT = PATCH_K // P
EC = E // P
PAIRS = HEADS // 2
MAXROWS = 2 * HEADS
SCALE = DH ** -0.5
EPS = 1e-5
OFF = -1e30
DIAG = -1e36
TAKEN = -3e38
TAKEN_BELOW = -2e38
assert MAXROWS + ROWS == P


class Image:

    def __init__(self, reg, off):
        self.reg, self.off = reg, off

    def count(self, per, k):
        c = self.off * per + k
        return c if self.reg is None else self.reg * (2 * per) + c

    def index(self):
        return self.off if self.reg is None else self.reg * 2 + self.off

    def back(self, n):
        return Image(self.reg, self.off - n)

    def exists(self):
        return self.reg is not None or self.off >= 0


class Ring:

    def __init__(self, banks, full, free, slots):
        self.banks, self.full, self.free = banks, full, free
        self.place, self.per = {}, [0] * len(banks)
        for n, name in enumerate(slots):
            b = n % len(banks)
            self.place[name] = (b, self.per[b])
            self.per[b] += 1

    def bank(self, name):
        return self.banks[self.place[name][0]]

    def full_of(self, name):
        return self.full[self.place[name][0]]

    def free_of(self, name):
        return self.free[self.place[name][0]]

    def emptied(self, name, img):
        b, k = self.place[name]
        return self.free[b], img.count(self.per[b], k)

    def holds(self, name, img):
        b, k = self.place[name]
        return self.full[b], img.count(self.per[b], k + 1)

    def gone(self, name, img):
        b, k = self.place[name]
        return self.free[b], img.count(self.per[b], k + 1)

    def all_gone(self, names, img):
        last = {}
        for name in sorted(names, key=lambda x: self.place[x][1]):
            last[self.place[name][0]] = name
        return [self.gone(name, img) for name in last.values()]


class Steps:

    def __init__(self, per):
        self.per, self.img, self.k = per, None, 0

    def begin(self, img):
        assert self.k in (0, self.per), (self.k, self.per)
        self.img, self.k = img, 0

    def next(self):
        self.k += 1
        return self.img.count(self.per, self.k)


def build(nc, xt, wtok, btok, wqkv, wout, bout, wfx, bfx, wxT, bx, wslice, bslice, temp,
          wqT2, wkT2, wvT2, wout2, bout2, identf, identb, diag, pick, out):
    fp32, bf16, fp16 = mybir.dt.float32, mybir.dt.bfloat16, mybir.dt.float16
    ALU, ACT, AX = mybir.AluOpType, mybir.ActivationFunctionType, mybir.AxisListType.X


    ctx = ExitStack()
    with ctx:
        def sb(name, shape, dt=fp32):
            return ctx.enter_context(nc.sbuf_tensor(name, shape, dt))

        def sem(name):
            return ctx.enter_context(nc.semaphore(name))

        consts = []

        def const(name, dram, dt=fp32):
            t = sb(name, list(dram.shape), dt)
            consts.append((t[:], dram))
            return t

        wtok_s = const("wtok_s", wtok)
        btok_s = const("btok_s", btok)
        wout_s = const("wout_s", wout)
        bout_s = const("bout_s", bout)
        bx_s = const("bx_s", bx)
        temp_s = const("temp_s", temp)
        bout2_s = const("bout2_s", bout2)
        identf_s = const("identf_s", identf)
        identb_s = const("identb_s", identb, bf16)
        diag_s = const("diag_s", diag, bf16)
        pick_s = const("pick_s", pick, bf16)
        ones_s = sb("ones_s", [P, P])
        half_s = sb("half_s", [P, NT])
        eps_s = sb("eps_s", [P, NT])
        wqkv_h, wqkv_l = sb("wqkv_h", [P, EC, 3 * INNER], fp16), sb("wqkv_l", [P, EC, 3 * INNER], fp16)
        wfx_h, wfx_l = sb("wfx_h", [P, EC, INNER], fp16), sb("wfx_l", [P, EC, INNER], fp16)
        wlog_h, wlog_l = sb("wlog_h", [P, EC, INNER], fp16), sb("wlog_l", [P, EC, INNER], fp16)
        bfx_rows, blog_rows = sb("bfx_rows", [P, INNER], fp16), sb("blog_rows", [P, INNER], fp16)
        ones_h = sb("ones_h", [P, ROWS], fp16)
        wqk_s = sb("wqk_s", [P, P])
        wvo_s = sb("wvo_s", [P, PAIRS, E])

        patches = sb("patches", [P, KT, NP])
        h = [sb(f"h{b}", [P, NT, E]) for b in range(2)]
        bn1 = sb("bn1", [P, NT, 6])
        mv1 = sb("mv1", [P, NT, 2])
        ve1 = sb("ve1", [P, NT])
        rstd1 = sb("rstd1", [P, NT])
        z = sb("z", [P, NT, E])
        zT_h, zT_l = sb("zT_h", [P, EC, NP], fp16), sb("zT_l", [P, EC, NP], fp16)
        early = sb("early", [P, 1024])
        zsq = early[:, 0:EC * NP].rearrange("p (c n) -> p c n", c=EC)
        x2 = sb("x2", [P, NP])
        scorebuf = sb("scorebuf", [P, NT * NP])
        score = scorebuf[:, :].rearrange("p (t n) -> p t n", t=NT)
        top8 = sb("top8", [P, NT, 8])
        mask = sb("mask", [P, NT, MAXROWS + NP], bf16)
        maskmax = sb("maskmax", [P, NT, NP], bf16)
        parts = {x: [sb(f"{x}_{y}", [P, PAIRS, NP], fp16) for y in "hl"] for x in "qk"}
        k_hl = sb("k_hl", [P, HEADS, NP], fp16)
        q_hl = sb("q_hl", [P, HEADS, NP], fp16)
        q_lh = sb("q_lh", [P, HEADS, NP], fp16)
        v1 = sb("v1", [P, NT, PAIRS, 2, P], fp16)
        v_l = sb("v_l", [P, NT, HEADS, DH], fp16)

        junk = [sb(f"junk{b}", [P, NP], bf16) for b in range(3)]
        mx = sb("mx", [P, NT, HEADS])
        maxhl = sb("maxhl", [P, NT, MAXROWS], bf16)
        heads = [sb(f"heads{b}", [P, NT * INNER]) for b in range(2)]
        probs = [x[:, 0:NT * NP].rearrange("p (t n) -> p t n", t=NT) for x in heads]
        probs_h = [sb(f"probs_h{b}", [P, NT, NP], fp16) for b in range(2)]
        probs_l = [sb(f"probs_l{b}", [P, NT, NP], fp16) for b in range(2)]
        rden = sb("rden", [P, 2, NP])
        oT = sb("oT", [P, PAIRS, NP])
        h2 = sb("h2", [P, NT, E])
        bn2 = sb("bn2", [P, NT, 6])
        mv2 = sb("mv2", [P, NT, 2])
        ve2 = sb("ve2", [P, NT])
        rstd2 = sb("rstd2", [P, NT])
        z2 = z
        z2T_h, z2T_l = [early[:, n * NP:(n + 1) * NP].bitcast(fp16).rearrange("p (c n) -> p c n", c=EC) for n in range(2)]
        fx = sb("fx", [P, NT, PAIRS, P + 1])
        logit, sw = [x[:, :].rearrange("p (t h g) -> p t h g", t=NT, h=HEADS) for x in heads]
        lmax = sb("lmax", [P, NT, HEADS])
        lsum = sb("lsum", [P, NT, HEADS])
        swT = oT
        snorm = sb("snorm", [P, PAIRS])
        token = sb("token", [P, PAIRS, P])
        late = [x[:, :, :].rearrange("p a b -> p (a b)").bitcast(fp32) for x in (*probs_h, *probs_l)]
        tokenT, tokenQ, attnT = [late[n][:, 0:PAIRS * P].rearrange("p (c k) -> p c k", c=PAIRS) for n in range(3)]
        tokenC = late[0][:, PAIRS * P:PAIRS * (P + SLICES)].rearrange("p (c k) -> p c k", c=PAIRS)
        ash, aexp = [late[3][:, n * 256:(n + 1) * 256].rearrange("p (c k) -> p c k", c=PAIRS) for n in range(2)]
        amax = sb("amax", [P, PAIRS])
        asum = sb("asum", [P, PAIRS])
        attn = sb("attn", [P, PAIRS, P])
        u = early[:, :].rearrange("p (c e) -> p c e", c=PAIRS)
        mix = scorebuf[:, 0:PAIRS * E].rearrange("p (c e) -> p c e", c=PAIRS)
        res = sb("res", [P, NT, E])

        wqk_f = heads[0][:, :].rearrange("p (c n) -> p c n", c=EC)
        wv_f, wfx_f = [heads[1][:, n * 1024:(n + 1) * 1024].rearrange("p (c n) -> p c n", c=EC) for n in range(2)]
        wxT_s = res[:, :, :]
        bslice_s = z[:, 0:2, :].rearrange("p a b -> p (a b)")
        bxrep = early[:, 0:PAIRS * P].rearrange("p (c k) -> p c k", c=PAIRS)
        wout2_s = h[0][:, :, :]
        bfx_s, blog_s = [rden[:, :, :].rearrange("p a b -> p (a b)")[:, 0:INNER], oT[:, 0:2, :].rearrange("p a b -> p (a b)")[:, 0:INNER]]
        wslice_s, wqT2_s, wkT2_s, wvT2_s = [scorebuf[:, n * P:(n + 1) * P] for n in range(4)]
        wlog_f = h[1][:, :, :].rearrange("p a b -> p (a b)").rearrange("p (c n) -> p c n", c=EC)
        consts += [(wqk_f, wqkv[:, :, 0:2 * INNER]), (wv_f, wqkv[:, :, 2 * INNER:]), (wfx_f, wfx), (wxT_s, wxT),
                   (bslice_s, bslice), (bfx_s, bfx), (wout2_s, wout2), (wslice_s, wslice), (wqT2_s, wqT2), (wkT2_s, wkT2),
                   (wvT2_s, wvT2)]

        def ring(name, n, slots):
            banks = [ctx.enter_context(nc.psum_tensor(f"{name}{b}", [P, 512], fp32)) for b in range(n)]
            return Ring(banks, [sem(f"{name}{b}_full") for b in range(n)],
                        [sem(f"{name}{b}_free") for b in range(n)], slots)

        T4, C4, H8 = range(NT), range(PAIRS), range(HEADS)
        front = ring("front", 2, [f"tok{t}" for t in T4] + ["zT0", "zT1", "x2"] + [f"gram{t}" for t in T4]
                     + [f"q{c}" for c in C4] + [f"k{c}" for c in C4] + ["v0", "v1"]
                     + [f"maskT{t}" for t in T4] + ["v2", "v3"])
        scores = ring("scores", 3, [f"s{t}_{hd}" for t in T4 for hd in H8]
                      + [f"sT{hd}_{t}" for hd in H8 for t in T4])
        rest = ring("rest", 3, ["maxT"] + [f"pv{hd}" for hd in H8]
                    + [f"proj{t}" for t in T4] + ["z2T0", "z2T1"] + [f"logit{t}" for t in T4]
                    + [f"fx{t}" for t in T4] + [f"swT{c}" for c in C4] + ["token0", "token1", "tokenT",
                    "tokenQ", "s2", "u0", "u1", "attnT", "mix0", "mix1"]
                    + [f"out{t}" for t in T4])

        consts_in = sem("consts_in")
        setup_vec = sem("setup_vec")
        setup_chain = sem("setup_chain")
        setup_pe = sem("setup_pe")
        setup_act = sem("setup_act")
        patches_in = sem("patches_in")
        q_stacked = sem("q_stacked")
        k_stacked = sem("k_stacked")
        out_stored = sem("out_stored")
        var1_ready = sem("var1_ready")
        var2_ready = sem("var2_ready")
        rstd1_ready = sem("rstd1_ready")
        rstd2_ready = sem("rstd2_ready")
        z_ready = sem("z_ready")
        z2_ready = sem("z2_ready")
        zT_high = sem("zT_high")
        z2T_high = sem("z2T_high")
        qk_high = sem("qk_high")
        v_high = sem("v_high")
        h_biased = sem("h_biased")
        h2_biased = sem("h2_biased")
        mask_ready = sem("mask_ready")
        maxhl_ready = sem("maxhl_ready")
        probs_split = sem("probs_split")
        pair_normed = sem("pair_normed")
        probs_ready = sem("probs_ready")
        logit_exped = sem("logit_exped")
        sw_ready = sem("sw_ready")
        attn_exped = sem("attn_exped")
        tokenT_whole = sem("tokenT_whole")
        maxima_placed = sem("maxima_placed")
        vec_tok_step = sem("vec_tok_step")
        attn_ready = sem("attn_ready")
        vec_knn_step = sem("vec_knn_step")
        vec_back_step = sem("vec_back_step")
        pool_root1_step = sem("pool_root1_step")
        pool_root2_step = sem("pool_root2_step")

        block = ctx.enter_context(nc.Block())

        def over_images(eng, body):
            body(None, None, Image(None, 0))
            body(None, Image(None, 0), Image(None, 1))
            body(Image(None, 0), Image(None, 1), Image(None, 2))
            with eng.Fori(0, BATCH // 2 - 2) as i:
                body(Image(i, 1), Image(i, 2), Image(i, 3))
                body(Image(i, 2), Image(i, 3), Image(i, 4))
            body(Image(None, BATCH - 3), Image(None, BATCH - 2), Image(None, BATCH - 1))
            body(Image(None, BATCH - 2), Image(None, BATCH - 1), None)
            body(Image(None, BATCH - 1), None, None)

        EARLY = 24
        TAIL = [range(n * EARLY // 6, (n + 1) * EARLY // 6) for n in range(6)]
        LATE = range(EARLY, EARLY + 3)
        HEAD = [range(EARLY + 3, EARLY + 5), range(EARLY + 5, EARLY + 7), range(EARLY + 7, NT * HEADS)]
        TOK_TAIL = [range(n * NT * KT // 6, (n + 1) * NT * KT // 6) for n in range(6)]
        TOK_WHOLE = [[t for t in T4 if (t + 1) * KT - 1 in steps] for steps in TOK_TAIL]

        def par(img):
            return img.off % 2

        @block.sync
        def _(sp):
            def take_wait():
                sp.nop(nofuse=True)

            for t, dram in consts:
                sp.dma_start(t, dram).then_inc(consts_in, 16)

            def load(F):
                if F.back(1).exists():
                    sp.wait_ge(*front.holds("tok3", F.back(1)))
                    take_wait()
                sp.dma_start(patches[:], xt[F.index()]).then_inc(patches_in, 16)

            def stack(x, done, F, high_over_low):
                lo, hi = slice(0, DH), slice(DH, P)
                sp.wait_ge(*front.gone(f"{x}{PAIRS - 2}", F))
                take_wait()
                sp.wait_ge(*front.gone(f"{x}{PAIRS - 1}", F))
                take_wait()
                for part, src in enumerate(parts[x]):
                    for dst, first in high_over_low:
                        rows = lo if part == first else hi
                        sp.dma_start(dst[rows, 0:HEADS:2, :], src[lo, :, :]).then_inc(done, 16)
                        sp.dma_start(dst[rows, 1:HEADS:2, :], src[hi, :, :]).then_inc(done, 16)

            def store(B):
                for t in range(1, NT):
                    sp.wait_ge(*rest.gone(f"out{t}", B))
                    take_wait()
                n = B.index()
                sp.dma_start(out[n, 0:3 * ROWS, :].rearrange("(t p) e -> p t e", p=ROWS),
                             res[0:ROWS, 0:3, :]).then_inc(out_stored, 16)
                sp.dma_start(out[n, 3 * ROWS:TOKENS, :], res[0:LAST, 3, :]).then_inc(out_stored, 16)

            def body(B, F, G):
                if G is not None:
                    load(G)
                if B is not None and B.back(1).exists():
                    store(B.back(1))
                if F is not None:
                    stack("q", q_stacked, F, [(q_hl, 0), (q_lh, 1)])
                    stack("k", k_stacked, F, [(k_hl, 0)])

            over_images(sp, body)
            store(Image(None, BATCH - 1))
            sp.wait_ge(out_stored, 32 * BATCH)

        @block.tensor
        def _(pe):
            mm = nc.tensor.matmul
            pe.wait_ge(consts_in, 16 * len(consts))
            pe.wait_ge(setup_vec, 2)
            for c in range(EC):
                for p in C4:
                    last = mm(scores.banks[c][:, p * P:(p + 1) * P], wxT_s[:, p, c * P:(c + 1) * P],
                              wslice_s, start=True, stop=True)
            for p in C4:
                last = mm(scores.banks[2][:, p * P:(p + 1) * P], bxrep[:, p, :], wslice_s,
                          start=True, stop=True)
            mm(front.banks[0][:, 0:P], wqT2_s, wkT2_s, start=True, stop=True)
            for p in C4:
                last = mm(rest.banks[p // 2][:, (p % 2) * E:(p % 2 + 1) * E], wvT2_s, wout2_s[:, p, :],
                          start=True, stop=True)
            last.then_inc(setup_pe, 1)
            pe.wait_ge(setup_vec, 3)
            pe.wait_ge(setup_act, 1)

            def split_product(out_, lhs, rhs, first=True, last=True):
                mm(out_, lhs[0], rhs[0], start=first, stop=False)
                mm(out_, lhs[0], rhs[1], start=False, stop=False)
                return mm(out_, lhs[1], rhs[0], start=False, stop=last)

            def tok(F, steps):
                for t, k in [divmod(n, KT) for n in steps]:
                    if (t, k) == (0, 0):
                        pe.wait_ge(patches_in, F.count(16, 16))
                    if k == 0:
                        pe.wait_ge(*front.emptied(f"tok{t}", F))
                    last = mm(front.bank(f"tok{t}")[0:ROWS, 0:E], patches[:, k, t * ROWS:(t + 1) * ROWS],
                              wtok_s[:, k, :], start=(k == 0), stop=(k == KT - 1))
                    if k == KT - 1:
                        last.then_inc(front.full_of(f"tok{t}"), 1)

            def transposes(ring_, names, img, src):
                for c, name in enumerate(names):
                    pe.wait_ge(*ring_.emptied(name, img))
                    bank = ring_.bank(name)
                    for t in T4:
                        last = nc.tensor.transpose(bank[:, t * ROWS:(t + 1) * ROWS],
                                                   src[0:ROWS, t, c * P:(c + 1) * P], identf_s[0:ROWS, 0:ROWS])
                    last.then_inc(ring_.full_of(name), 1)

            def ztr(F):
                pe.wait_ge(z_ready, F.count(1, 1))
                transposes(front, ["zT0", "zT1"], F, z)

            def norms(F):
                for sem_, n in front.all_gone(["zT0", "zT1"], F):
                    pe.wait_ge(sem_, n)
                pe.wait_ge(*front.emptied("x2", F))
                bank = front.bank("x2")
                for c in range(EC):
                    last = mm(bank[0:ROWS, 0:NP], ones_s[:, 0:ROWS], zsq[:, c, :], start=(c == 0), stop=(c == 1))
                last.then_inc(front.full_of("x2"), 1)

            def gram(F, ts):
                for t in ts:
                    pe.wait_ge(*front.emptied(f"gram{t}", F))
                    bank = front.bank(f"gram{t}")
                    rows = slice(t * ROWS, (t + 1) * ROWS)
                    for c in range(EC):
                        split_product(bank[0:ROWS, 0:NP], (zT_h[:, c, rows], zT_l[:, c, rows]),
                                      (zT_h[:, c, :], zT_l[:, c, :]), first=(c == 0), last=False)
                    last = mm(bank[0:ROWS, 0:NP], identb_s[0:ROWS, 0:ROWS], diag_s[0:ROWS, t, :],
                              start=False, stop=True)
                    last.then_inc(front.full_of(f"gram{t}"), 1)

            def qk(F, which, ps):
                base = {"q": 0, "k": INNER}[which]
                for p in ps:
                    pe.wait_ge(*front.emptied(f"{which}{p}", F))
                    bank = front.bank(f"{which}{p}")
                    cols = slice(base + p * P, base + (p + 1) * P)
                    for c in range(EC):
                        last = split_product(bank[:, 0:NP], (wqkv_h[:, c, cols], wqkv_l[:, c, cols]),
                                             (zT_h[:, c, :], zT_l[:, c, :]), first=(c == 0), last=(c == 1))
                    last.then_inc(front.full_of(f"{which}{p}"), 1)

            def vals(F, ts):
                for t in ts:
                    pe.wait_ge(*front.emptied(f"v{t}", F))
                    bank = front.bank(f"v{t}")
                    rows = slice(t * ROWS, (t + 1) * ROWS)
                    for c in range(EC):
                        last = split_product(bank[0:ROWS, :], (zT_h[:, c, rows], zT_l[:, c, rows]),
                                             (wqkv_h[:, c, 2 * INNER:], wqkv_l[:, c, 2 * INNER:]),
                                             first=(c == 0), last=(c == 1))
                    last.then_inc(front.full_of(f"v{t}"), 1)

            def mask_tr(F, ts):
                if ts[0] == 0:
                    pe.wait_ge(mask_ready, F.count(1, 1))
                for mt in ts:
                    pe.wait_ge(*front.emptied(f"maskT{mt}", F))
                    bank = front.bank(f"maskT{mt}").bitcast(bf16)
                    for t in T4:
                        last = nc.tensor.transpose(bank[:, t * ROWS:(t + 1) * ROWS],
                                                   mask[0:ROWS, t, mt * ROWS:mt * ROWS + P],
                                                   identb_s[0:ROWS, 0:ROWS])
                    last.then_inc(front.full_of(f"maskT{mt}"), 1)

            def score_rows(B, tiles):
                for t, hd in [divmod(n, HEADS) for n in tiles]:
                    if (t, hd) == (0, 0):
                        pe.wait_ge(q_stacked, B.count(128, 128))
                        pe.wait_ge(k_stacked, B.count(64, 64))
                    pe.wait_ge(*scores.emptied(f"s{t}_{hd}", B))
                    bank = scores.bank(f"s{t}_{hd}")
                    mm(bank[0:ROWS, 0:NP], q_hl[:, hd, t * ROWS:(t + 1) * ROWS], k_hl[:, hd, :],
                       start=True, stop=True).then_inc(scores.full_of(f"s{t}_{hd}"), 1)

            def max_tr(B):
                pe.wait_ge(maxhl_ready, B.count(1, 1))
                pe.wait_ge(*rest.emptied("maxT", B))
                bank = rest.bank("maxT").bitcast(bf16)
                for t in T4:
                    last = nc.tensor.transpose(bank[0:MAXROWS, t * ROWS:(t + 1) * ROWS],
                                               maxhl[0:ROWS, t, :], identb_s[0:ROWS, 0:ROWS])
                last.then_inc(rest.full_of("maxT"), 1)

            def score_cols(B, hd):
                if hd == 0:
                    for sem_, n in front.all_gone([f"maskT{t}" for t in T4], B):
                        pe.wait_ge(sem_, n)
                for ts in ([T4[0:3], T4[3:]] if hd == 0 else [[t] for t in T4]):
                    for t in ts:
                        pe.wait_ge(*scores.emptied(f"sT{hd}_{t}", B))
                        bank = scores.bank(f"sT{hd}_{t}")
                        k_ = k_hl[:, hd, t * ROWS:(t + 1) * ROWS]
                        mm(bank[0:ROWS, 0:NP], k_, q_hl[:, hd, :], start=True, stop=False)
                        mm(bank[0:ROWS, 0:NP], k_, q_lh[:, hd, :], start=False, stop=False)
                    for t in ts:
                        if hd == 0 and t < NT - 1:
                            pe.wait_ge(maxima_placed, B.count(NT - 1, t + 1))
                        elif hd == 0:
                            pe.wait_ge(*rest.gone("maxT", B))
                        bank = scores.bank(f"sT{hd}_{t}")
                        mm(bank[0:ROWS, 0:NP], pick_s[:, hd, :], maskmax[:, t, :], start=False, stop=True)\
                            .then_inc(scores.full_of(f"sT{hd}_{t}"), 1)

            def pv(B, hd):
                if hd == 0:
                    for sem_, n in front.all_gone([f"v{t}" for t in T4], B):
                        pe.wait_ge(sem_, n)
                pe.wait_ge(*rest.emptied(f"pv{hd}", B))
                bank = rest.bank(f"pv{hd}")
                b, own = hd % 2, slice((hd % 2) * DH, (hd % 2 + 1) * DH)
                for sem_, n in scores.all_gone([f"sT{hd}_{t}" for t in T4], B):
                    pe.wait_ge(sem_, n)
                for m in T4:
                    mm(bank[:, 0:NP], v1[0:ROWS, m, hd // 2, hd % 2, :], probs_h[b][0:ROWS, m, :],
                       start=(m == 0), stop=False)
                for m in T4:
                    mm(bank[own, 0:NP], v_l[0:ROWS, m, hd, :], probs_h[b][0:ROWS, m, :], start=False, stop=False)
                for m in T4:
                    pe.wait_ge(probs_ready, B.count(HEADS * NT, hd * NT + m + 1))
                    last = mm(bank[:, 0:NP], v1[0:ROWS, m, hd // 2, hd % 2, :], probs_l[b][0:ROWS, m, :],
                              start=False, stop=(m == NT - 1))
                last.then_inc(rest.full_of(f"pv{hd}"), 1)

            def rows_product(B, name, ts, srcT, w, n):
                chunks = srcT.shape[1]
                for t in ts:
                    pe.wait_ge(*rest.emptied(f"{name}{t}", B))
                    bank = rest.bank(f"{name}{t}")
                    for c in range(chunks):
                        last = mm(bank[0:ROWS, 0:n], srcT[:, c, t * ROWS:(t + 1) * ROWS], w[:, c, :],
                                  start=(c == 0), stop=(c == chunks - 1))
                    last.then_inc(rest.full_of(f"{name}{t}"), 1)

            def proj(B):
                pe.wait_ge(pair_normed, B.count(PAIRS + 1, PAIRS))
                rows_product(B, "proj", T4[0:NT // 2], oT, wout_s, E)
                pe.wait_ge(pair_normed, B.count(PAIRS + 1, PAIRS + 1))
                rows_product(B, "proj", T4[NT // 2:], oT, wout_s, E)

            def ffn_transpose(B):
                pe.wait_ge(z2_ready, B.count(1, 1))
                transposes(rest, ["z2T0", "z2T1"], B, z2)

            def ffn_in(B, which, w_h, w_l, bias_rows, ts):
                if which == "logit":
                    for sem_, n in rest.all_gone(["z2T0", "z2T1"], B):
                        pe.wait_ge(sem_, n)
                for t in ts:
                    pe.wait_ge(*rest.emptied(f"{which}{t}", B))
                    bank = rest.bank(f"{which}{t}")
                    rows = slice(t * ROWS, (t + 1) * ROWS)
                    for c in range(EC):
                        split_product(bank[0:ROWS, :], (z2T_h[:, c, rows], z2T_l[:, c, rows]),
                                      (w_h[:, c, :], w_l[:, c, :]), first=(c == 0), last=False)
                    last = mm(bank[0:ROWS, :], ones_h[:], bias_rows[:], start=False, stop=True)
                    last.then_inc(rest.full_of(f"{which}{t}"), 1)

            def sw_tr(B):
                pe.wait_ge(sw_ready, B.count(NT, NT))
                for c in C4:
                    pe.wait_ge(*rest.emptied(f"swT{c}", B))
                    bank = rest.bank(f"swT{c}")
                    for t in T4:
                        last = nc.tensor.transpose(bank[:, t * ROWS:(t + 1) * ROWS],
                                                   sw[0:ROWS, t, 2 * c:2 * c + 2, :], identf_s[0:ROWS, 0:ROWS])
                    last.then_inc(rest.full_of(f"swT{c}"), 1)

            def tokens(B):
                for sem_, n in rest.all_gone(["swT1", *[f"fx{t}" for t in T4]], B):
                    pe.wait_ge(sem_, n)
                for g in range(2):
                    pe.wait_ge(*rest.emptied(f"token{g}", B))
                    bank = rest.bank(f"token{g}")
                    for j in range(2):
                        p = 2 * g + j
                        for t in T4:
                            n = ROWS if t < NT - 1 else LAST
                            last = mm(bank[:, j * (P + 1):(j + 1) * (P + 1)], sw[0:n, t, 2 * p:2 * p + 2, :],
                                      fx[0:n, t, p, :], start=(t == 0), stop=(t == NT - 1))
                    last.then_inc(rest.full_of(f"token{g}"), 1)

            def square_tr(B, src, name):
                pe.wait_ge(*rest.emptied(name, B))
                bank = rest.bank(name)
                for p in C4:
                    last = nc.tensor.transpose(bank[:, p * P:(p + 1) * P], src[:, p, :], identf_s[:])
                last.then_inc(rest.full_of(name), 1)

            def token_tr(B):
                for sem_, n in rest.all_gone(["token0", "token1"], B):
                    pe.wait_ge(sem_, n)
                square_tr(B, token, "tokenT")

            def token_q(B):
                pe.wait_ge(tokenT_whole, B.count(1, 1))
                pe.wait_ge(*rest.emptied("tokenQ", B))
                mm(rest.bank("tokenQ")[:, :], wqk_s[:], tokenT[:, :, :], start=True, stop=True)\
                    .then_inc(rest.full_of("tokenQ"), 1)

            def token_scores(B):
                pe.wait_ge(*rest.gone("tokenT", B))
                pe.wait_ge(*rest.gone("tokenQ", B))
                pe.wait_ge(*rest.emptied("s2", B))
                bank = rest.bank("s2")
                for p in C4:
                    last = mm(bank[:, p * SLICES:(p + 1) * SLICES], tokenQ[:, p, :], tokenC[:, p, :],
                              start=True, stop=True)
                last.then_inc(rest.full_of("s2"), 1)

            def paired(B, names, lhs, rhs):
                for g in range(2):
                    pe.wait_ge(*rest.emptied(names[g], B))
                    bank = rest.bank(names[g])
                    for j in range(2):
                        p = 2 * g + j
                        last = mm(bank[:, j * E:(j + 1) * E], lhs[:, p, :], rhs[:, p, :], start=True, stop=True)
                    last.then_inc(rest.full_of(names[g]), 1)

            def body(B, F, G):
                if B is not None:
                    score_rows(B, HEAD[0])
                if F is not None:
                    norms(F)
                    gram(F, [0])
                if B is not None:
                    score_rows(B, HEAD[1])
                if F is not None:
                    gram(F, [1])
                if B is not None:
                    score_rows(B, HEAD[2])
                if F is not None:
                    gram(F, [2])
                if B is not None:
                    max_tr(B)
                if F is not None:
                    gram(F, [3])
                if B is not None:
                    score_cols(B, 0)
                    for hd in range(1, HEADS - 2):
                        score_cols(B, hd)
                        pv(B, hd - 1)
                for n in range(2):
                    if B is not None:
                        score_cols(B, HEADS - 2 + n)
                    if F is not None:
                        qk(F, "q", [n])
                    if B is not None:
                        pv(B, HEADS - 3 + n)
                if B is not None:
                    pv(B, HEADS - 1)
                if F is not None:
                    qk(F, "q", [2, 3])
                if B is not None:
                    proj(B)
                if F is not None:
                    qk(F, "k", C4)
                if B is not None:
                    ffn_transpose(B)
                if F is not None:
                    vals(F, [0, 1])
                if B is not None:
                    ffn_in(B, "logit", wlog_h, wlog_l, blog_rows, T4)
                for t in T4:
                    if B is not None:
                        ffn_in(B, "fx", wfx_h, wfx_l, bfx_rows, [t])
                    if F is not None:
                        mask_tr(F, [t])
                if F is not None:
                    vals(F, [2, 3])
                if B is not None:
                    sw_tr(B)
                    tokens(B)
                for n in range(6):
                    for k in range(4):
                        if F is not None:
                            score_rows(F, TAIL[n][k:k + 1])
                        if G is not None:
                            tok(G, TOK_TAIL[n][k:k + 1])
                    if B is not None and n == 0:
                        token_tr(B)
                    if B is not None and n == 1:
                        token_q(B)
                    if B is not None and n == 2:
                        token_scores(B)
                        paired(B, ["u0", "u1"], tokenT, wvo_s)
                    if B is not None and n == 3:
                        pe.wait_ge(attn_ready, B.count(1, 1))
                        square_tr(B, attn, "attnT")
                    if B is not None and n == 4:
                        for sem_, m in rest.all_gone(["attnT", "u0", "u1"], B):
                            pe.wait_ge(sem_, m)
                        paired(B, ["mix0", "mix1"], attnT, u)
                if B is not None:
                    for sem_, n in rest.all_gone(["attnT", "mix0", "mix1"], B):
                        pe.wait_ge(sem_, n)
                    rows_product(B, "out", T4[0:3], swT, mix, E)
                if F is not None:
                    score_rows(F, LATE)
                if G is not None:
                    ztr(G)
                if B is not None:
                    rows_product(B, "out", T4[3:], swT, mix, E)

            over_images(pe, body)

        @block.scalar
        def _(act):
            A = nc.scalar.activation

            act.wait_ge(consts_in, 16 * len(consts))
            A(wqkv_h[:, :, 0:2 * INNER], wqk_f, ACT.Copy)
            A(wqkv_h[:, :, 2 * INNER:], wv_f, ACT.Copy)
            A(wfx_h[:], wfx_f, ACT.Copy).then_inc(setup_act, 1)

            def copy(ring_, name, img, dst, width=None, src=None):
                act.wait_ge(*ring_.holds(name, img))
                bank = ring_.bank(name)
                A(dst, bank[:, 0:width] if src is None else src(bank), ACT.Copy).then_inc(ring_.free_of(name), 1)

            def front_transposed(F):
                for c in range(EC):
                    act.wait_ge(*front.holds(f"zT{c}", F))
                    bank = front.bank(f"zT{c}")
                    A(zsq[:, c, :], bank[:, 0:NP], ACT.Square)
                    A(zT_h[:, c, :], bank[:, 0:NP], ACT.Copy).then_inc(zT_high, 1)

            def norms(F):
                act.wait_ge(*front.holds("x2", F))
                if F.back(1).exists():
                    act.wait_ge(*front.gone("gram3", F.back(1)))
                A(x2[0:ROWS, :], front.bank("x2")[0:ROWS, 0:NP], ACT.Copy).then_inc(front.free_of("x2"), 1)

            def qk(F, which, ps):
                for p in ps:
                    act.wait_ge(*front.holds(f"{which}{p}", F))
                    A(parts[which][0][:, p, :], front.bank(f"{which}{p}")[:, 0:NP], ACT.Copy).then_inc(qk_high, 1)

            def vals(F, ts):
                for t in ts:
                    act.wait_ge(*front.holds(f"v{t}", F))
                    bank = front.bank(f"v{t}")[0:ROWS, :].rearrange("p (c j d) -> p c j d", c=PAIRS, j=2)
                    A(v1[0:ROWS, t, :, 0, 0:DH], bank[:, :, 0, :], ACT.Copy)
                    A(v1[0:ROWS, t, :, 1, DH:P], bank[:, :, 1, :], ACT.Copy).then_inc(v_high, 1)

            def masks(F, ts):
                for t in ts:
                    copy(front, f"maskT{t}", F, maskmax[:, t, :], src=lambda bank: bank.bitcast(bf16)[:, 0:NP])

            def maxima(B):
                act.wait_ge(*rest.holds("maxT", B))
                bank = rest.bank("maxT").bitcast(bf16)
                for t in T4[0:NT - 1]:
                    A(maskmax[0:MAXROWS, t, :], bank[0:MAXROWS, 0:NP], ACT.Copy).then_inc(maxima_placed, 1)
                A(maskmax[0:MAXROWS, NT - 1, :], bank[0:MAXROWS, 0:NP], ACT.Copy).then_inc(rest.free_of("maxT"), 1)

            def exps(B, hd, ts=T4):
                for t in ts:
                    act.wait_ge(*scores.holds(f"sT{hd}_{t}", B))
                    bank = scores.bank(f"sT{hd}_{t}")[0:ROWS, 0:NP]
                    A(probs[hd % 2][0:ROWS, t, :], bank, ACT.Exp, scale=SCALE).then_inc(probs_split, 1)
                    A(probs_h[hd % 2][0:ROWS, t, :], bank, ACT.Exp, scale=SCALE)\
                        .then_inc(scores.free_of(f"sT{hd}_{t}"), 1)

            def outputs_and_sums(B, hd):
                own, other = slice((hd % 2) * DH, (hd % 2 + 1) * DH), slice((1 - hd % 2) * DH, (2 - hd % 2) * DH)
                p = hd // 2
                if hd % 2 == 0 and p >= 2:
                    act.wait_ge(pair_normed, B.count(PAIRS + 1, p - 1))
                act.wait_ge(*rest.holds(f"pv{hd}", B))
                bank = rest.bank(f"pv{hd}")
                A(oT[own, p, :], bank[own, 0:NP], ACT.Copy)
                last = A(rden[own, p % 2, :], bank[other, 0:NP], ACT.Copy)
                last.then_inc(rest.free_of(f"pv{hd}"), 1)

            def body(B, F, G):
                if F is not None:
                    norms(F)
                if B is not None:
                    maxima(B)
                    exps(B, 0)
                    exps(B, 1)
                    for hd in range(2, HEADS - 2):
                        exps(B, hd)
                        outputs_and_sums(B, hd - 2)
                if B is not None:
                    exps(B, HEADS - 2)
                if F is not None:
                    qk(F, "q", [0])
                if B is not None:
                    outputs_and_sums(B, HEADS - 4)
                    exps(B, HEADS - 1, T4[0:2])
                    outputs_and_sums(B, HEADS - 3)
                    exps(B, HEADS - 1, T4[2:])
                if F is not None:
                    qk(F, "q", [1])
                if B is not None:
                    outputs_and_sums(B, HEADS - 2)
                    outputs_and_sums(B, HEADS - 1)
                if F is not None:
                    qk(F, "q", [2, 3])
                    qk(F, "k", C4)
                if B is not None:
                    for c in range(EC):
                        act.wait_ge(*rest.holds(f"z2T{c}", B))
                        A(z2T_h[:, c, :], rest.bank(f"z2T{c}")[:, 0:NP], ACT.Copy).then_inc(z2T_high, 1)
                if F is not None:
                    vals(F, [0, 1])
                for t in T4:
                    if B is not None:
                        act.wait_ge(*rest.gone(f"logit{t}", B))
                        A(sw[0:ROWS, t, :, :], logit[0:ROWS, t, :, :], ACT.Exp).then_inc(logit_exped, 1)
                        copy(rest, f"fx{t}", B, fx[0:ROWS, t, :, 0:P],
                             src=lambda bank: bank[0:ROWS, :].rearrange("p (c k) -> p c k", c=PAIRS))
                    if F is not None:
                        masks(F, [t])
                if F is not None:
                    vals(F, [2, 3])
                if B is not None:
                    for c in C4:
                        copy(rest, f"swT{c}", B, swT[:, c, :], NP)
                    act.wait_ge(*rest.holds("tokenT", B))
                    bank = rest.bank("tokenT")[:, :].rearrange("p (c k) -> p c k", c=PAIRS)
                    A(tokenT[:, :, :], bank, ACT.Copy).then_inc(tokenT_whole, 1)
                    A(tokenC[0:DH, :, :], bank[0:DH, :, 0:SLICES], ACT.Copy)
                    A(tokenC[DH:P, :, :], bank[DH:P, :, SLICES:P], ACT.Copy).then_inc(rest.free_of("tokenT"), 1)
                    copy(rest, "tokenQ", B, tokenQ[:, :, :], 512)
                    act.wait_ge(*rest.gone("s2", B))
                    A(aexp[:, :, :], ash[:, :, :], ACT.Exp, scale=SCALE).then_inc(attn_exped, 1)
                    for g in range(2):
                        copy(rest, f"u{g}", B, u[:, 2 * g:2 * g + 2, :], 512)
                    copy(rest, "attnT", B, attnT[:, :, :], 512)
                    for g in range(2):
                        copy(rest, f"mix{g}", B, mix[:, 2 * g:2 * g + 2, :], 512)
                if G is not None:
                    front_transposed(G)

            over_images(act, body)

        @block.vector
        def _(dve):
            V = nc.vector

            def take_wait():
                dve.nop(nofuse=True)

            back_step = Steps(1 + PAIRS + 1 + 1 + 3 * NT + 4 + 3)
            knn_step = Steps(NT * 2 * (KNN // 8))
            tok_step = Steps(1)

            def low_part(dst, x, high):
                return V.tensor_tensor(dst, x, high, ALU.subtract)

            V.memset(ones_s[:], 1.0)
            V.memset(ones_h[:], 1.0)
            V.memset(bfx_rows[:], 0.0)
            V.memset(blog_rows[:], 0.0)
            V.memset(half_s[:], -0.5)
            V.memset(eps_s[:], EPS)
            V.memset(mask[:, :, 0:MAXROWS], 0.0)
            V.memset(v1[:], 1.0)
            V.memset(fx[:, :, :, P:P + 1], 1.0)
            V.memset(token[:], 0.0)
            V.memset(attn[:], 0.0).then_inc(setup_vec, 1)
            dve.wait_ge(consts_in, 16 * len(consts))
            V.tensor_scalar(temp_s[:], temp_s[:], 0.1, 5.0, ALU.max, ALU.min).then_inc(setup_chain, 1)
            V.tensor_copy(bxrep, bx_s[:, :].unsqueeze(2).to_broadcast([P, PAIRS, P])).then_inc(setup_vec, 1)
            dve.wait_ge(setup_chain, 1)
            V.reciprocal(temp_s[:], temp_s[:]).then_inc(setup_chain, 1)
            dve.wait_ge(setup_act, 1)
            low_part(wqkv_l[:, :, 0:2 * INNER], wqk_f, wqkv_h[:, :, 0:2 * INNER])
            low_part(wqkv_l[:, :, 2 * INNER:], wv_f, wqkv_h[:, :, 2 * INNER:])
            low_part(wfx_l[:], wfx_f, wfx_h[:])
            dve.wait_ge(setup_chain, 2)
            invt = temp_s[:, :].unsqueeze(2).to_broadcast([P, HEADS, SLICES])
            dve.wait_ge(setup_pe, 1)
            V.tensor_copy(wqk_s[:], front.banks[0][:, 0:P])
            for g in range(2):
                V.tensor_copy(wvo_s[:, 2 * g:2 * g + 2, :], rest.banks[g][:, :].rearrange("p (c e) -> p c e", c=2))
            V.tensor_tensor(blog_s, scores.banks[2][:, :], bslice_s, ALU.add)
            V.tensor_copy(bfx_rows[0:1, :], bfx_s[0:1, :])
            for c in range(EC):
                last = V.tensor_tensor(wlog_f[:, c, :].rearrange("p (h g) -> p h g", h=HEADS),
                                       scores.banks[c][:, :].rearrange("p (h g) -> p h g", h=HEADS), invt, ALU.mult)
            last.then_inc(setup_chain, 1)
            dve.wait_ge(setup_chain, 3)
            V.tensor_copy(wlog_h[:], wlog_f).then_inc(setup_chain, 1)
            V.tensor_tensor(blog_s.rearrange("p (h g) -> p h g", h=HEADS),
                            blog_s.rearrange("p (h g) -> p h g", h=HEADS), invt, ALU.mult).then_inc(setup_chain, 1)
            dve.wait_ge(setup_chain, 5)
            V.tensor_copy(blog_rows[0:1, :], blog_s[0:1, :]).then_inc(setup_chain, 1)
            low_part(wlog_l[:], wlog_f, wlog_h[:])
            low_part(bfx_rows[32:33, :], bfx_s[0:1, :], bfx_rows[0:1, :])
            dve.wait_ge(setup_chain, 6)
            low_part(blog_rows[32:33, :], blog_s[0:1, :], blog_rows[0:1, :]).then_inc(setup_vec, 1)
            dve.wait_ge(setup_vec, 3)

            def stats(ring_, name, img, src, bn, t, step_sem):
                dve.wait_ge(*ring_.gone(f"{name}{t}", img))
                last = V.bn_stats(bn[0:ROWS, t, :], src[0:ROWS, t, :])
                if t == NT - 1:
                    last.then_inc(step_sem, 1)

            def moments(steps, step_sem, bn, mv, var_sem):
                dve.wait_ge(step_sem, steps.next())
                take_wait()
                for t in T4:
                    last = V.bn_aggr(mv[0:ROWS, t, :], bn[0:ROWS, t, :])
                last.then_inc(var_sem, 1)

            def normed(img, src, mv, dst, rstd, rstd_sem, dst_sem):
                dve.wait_ge(rstd_sem, img.count(1, 1))
                for t in T4:
                    last = V.tensor_scalar(dst[0:ROWS, t, :], src[0:ROWS, t, :], mv[0:ROWS, t, 0:1],
                                           rstd[0:ROWS, t:t + 1], ALU.subtract, ALU.mult)
                last.then_inc(dst_sem, 1)

            def tok(F, ts):
                for t in ts:
                    dve.wait_ge(*front.holds(f"tok{t}", F))
                    V.tensor_tensor(h[par(F)][0:ROWS, t, :], front.bank(f"tok{t}")[0:ROWS, 0:E],
                                    btok_s[0:ROWS, :], ALU.add).then_inc(front.free_of(f"tok{t}"), 1)
                    stats(front, "tok", F, h[par(F)], bn1, t, vec_tok_step)

            def tok_norm(F):
                tok_step.begin(F)
                moments(tok_step, vec_tok_step, bn1, mv1, var1_ready)
                normed(F, h[par(F)], mv1, z, rstd1, rstd1_ready, z_ready)

            def low_transposed(ring_, name, high_sem, low, high, img):
                for c in range(EC):
                    dve.wait_ge(high_sem, img.count(EC, c + 1))
                    low_part(low[:, c, :], ring_.bank(f"{name}{c}")[:, 0:NP], high[:, c, :])\
                        .then_inc(ring_.free_of(f"{name}{c}"), 1)

            def gram(F, ts):
                for t in ts:
                    if t == 0:
                        dve.wait_ge(*front.gone("x2", F))
                    dve.wait_ge(*front.holds(f"gram{t}", F))
                    V.scalar_tensor_tensor(out=score[0:ROWS, t, :], in0=front.bank(f"gram{t}")[0:ROWS, 0:NP],
                                           scalar=2.0, in1=x2[0:ROWS, :], op0=ALU.mult,
                                           op1=ALU.subtract).then_inc(front.free_of(f"gram{t}"), 1)

            def neighbours(F, ts):
                if ts[0] == 0:
                    knn_step.begin(F)
                for t in ts:
                    dve.wait_ge(*front.gone(f"gram{t}", F))
                taken = {}
                for r in range(KNN // 8):
                    found = {}
                    for t in ts:
                        if r > 0:
                            dve.wait_ge(vec_knn_step, taken[t])
                        take_wait()
                        V.max(out=top8[0:ROWS, t, :], in_=score[0:ROWS, t, :]).then_inc(vec_knn_step, 1)
                        found[t] = knn_step.next()
                    for t in ts:
                        dve.wait_ge(vec_knn_step, found[t])
                        take_wait()
                        V.match_replace(out=score[0:ROWS, t, :], in_to_replace=top8[0:ROWS, t, :],
                                        in_values=score[0:ROWS, t, :], imm_value=TAKEN).then_inc(vec_knn_step, 1)
                        taken[t] = knn_step.next()
                for t in ts:
                    dve.wait_ge(vec_knn_step, taken[t])
                    last = V.tensor_scalar(mask[0:ROWS, t, MAXROWS:], score[0:ROWS, t, :], TAKEN_BELOW, OFF,
                                           ALU.is_gt, ALU.mult)
                if ts[-1] == NT - 1:
                    last.then_inc(mask_ready, 1)

            def low_qk(F, which, ps):
                for p in ps:
                    dve.wait_ge(qk_high, F.count(2 * PAIRS, "qk".index(which) * PAIRS + p + 1))
                    low_part(parts[which][1][:, p, :], front.bank(f"{which}{p}")[:, 0:NP],
                             parts[which][0][:, p, :]).then_inc(front.free_of(f"{which}{p}"), 1)

            def low_vals(F, ts):
                for t in ts:
                    dve.wait_ge(v_high, F.count(NT, t + 1))
                    bank = front.bank(f"v{t}")[0:ROWS, :].rearrange("p (c j d) -> p c j d", c=PAIRS, j=2)
                    low = v_l[0:ROWS, t, :, :].rearrange("p (c j) d -> p c j d", j=2)
                    low_part(low[:, :, 0, :], bank[:, :, 0, :], v1[0:ROWS, t, :, 0, 0:DH])
                    low_part(low[:, :, 1, :], bank[:, :, 1, :], v1[0:ROWS, t, :, 1, DH:P])\
                        .then_inc(front.free_of(f"v{t}"), 1)

            def row_maxima(B, tiles):
                for t, hd in [divmod(n, HEADS) for n in tiles]:
                    name = f"s{t}_{hd}"
                    if (t, hd) == (0, 0):
                        dve.wait_ge(mask_ready, B.count(1, 1))
                    dve.wait_ge(*scores.holds(name, B))
                    take_wait()
                    V.tensor_tensor_reduce(
                        out=junk[scores.place[name][0]][0:ROWS, :], in0=scores.bank(name)[0:ROWS, 0:NP],
                        in1=mask[0:ROWS, t, MAXROWS:], scale=1.0, scalar=-3e38, op0=ALU.add, op1=ALU.max,
                        accum_out=mx[0:ROWS, t, hd:hd + 1]).then_inc(scores.free_of(name), 1)

            def maxima_parts(B):
                back_step.begin(B)
                for sem_, n in scores.all_gone([f"s{NT - 1}_{hd}" for hd in H8], B):
                    dve.wait_ge(sem_, n)
                V.tensor_scalar(maxhl[0:ROWS, :, 0:HEADS], mx[0:ROWS, :, :], -1.0, None, ALU.mult)\
                    .then_inc(vec_back_step, 1)
                dve.wait_ge(vec_back_step, back_step.next())
                V.scalar_tensor_tensor(out=maxhl[0:ROWS, :, HEADS:MAXROWS], in0=mx[0:ROWS, :, :], scalar=-1.0,
                                       in1=maxhl[0:ROWS, :, 0:HEADS], op0=ALU.mult, op1=ALU.subtract)\
                 .then_inc(maxhl_ready, 1)

            def norm(B, p):
                dve.wait_ge(*rest.gone(f"pv{2 * p}", B))
                dve.wait_ge(*rest.gone(f"pv{2 * p + 1}", B))
                for cols in ([slice(0, NP)] if p < PAIRS - 1 else [slice(0, NP // 2), slice(NP // 2, NP)]):
                    V.reciprocal(rden[:, p % 2, cols], rden[:, p % 2, cols]).then_inc(vec_back_step, 1)
                    dve.wait_ge(vec_back_step, back_step.next())
                    V.tensor_tensor(oT[:, p, cols], oT[:, p, cols], rden[:, p % 2, cols], ALU.mult)\
                        .then_inc(pair_normed, 1)

            def proj(B):
                dve.wait_ge(h_biased, B.count(1, 1))
                for t in T4:
                    dve.wait_ge(*rest.holds(f"proj{t}", B))
                    V.tensor_tensor(h2[0:ROWS, t, :], rest.bank(f"proj{t}")[0:ROWS, 0:E], h[par(B)][0:ROWS, t, :],
                                    ALU.add).then_inc(rest.free_of(f"proj{t}"), 1)
                    stats(rest, "proj", B, h2, bn2, t, vec_back_step)
                moments(back_step, vec_back_step, bn2, mv2, var2_ready)

            def wide(x, t):
                return x[0:ROWS, t, :].unsqueeze(2).to_broadcast([ROWS, HEADS, SLICES])

            def ffn_shift(B):
                for t in T4:
                    dve.wait_ge(*rest.holds(f"logit{t}", B))
                    bank = rest.bank(f"logit{t}")[0:ROWS, :].rearrange("p (h g) -> p h g", h=HEADS)
                    V.tensor_reduce(lmax[0:ROWS, t, :], bank, AX, ALU.max).then_inc(vec_back_step, 1)
                    dve.wait_ge(vec_back_step, back_step.next())
                    V.tensor_tensor(logit[0:ROWS, t, :, :], bank, wide(lmax, t), ALU.subtract)\
                        .then_inc(rest.free_of(f"logit{t}"), 1)

            def ffn_softmax(B):
                for t in T4:
                    st = sw[0:ROWS, t, :, :]
                    dve.wait_ge(logit_exped, B.count(NT, t + 1))
                    V.tensor_reduce(lsum[0:ROWS, t, :], st, AX, ALU.add).then_inc(vec_back_step, 1)
                    dve.wait_ge(vec_back_step, back_step.next())
                    V.reciprocal(lsum[0:ROWS, t, :], lsum[0:ROWS, t, :]).then_inc(vec_back_step, 1)
                    dve.wait_ge(vec_back_step, back_step.next())
                    V.tensor_tensor(st, st, wide(lsum, t), ALU.mult).then_inc(sw_ready, 1)

            def tokens(B):
                for g in range(2):
                    dve.wait_ge(*rest.holds(f"token{g}", B))
                    bank = rest.bank(f"token{g}")[:, 0:2 * (P + 1)].rearrange("p (c k) -> p c k", c=2)
                    n = snorm[:, 2 * g:2 * g + 2]
                    V.tensor_scalar(n, bank[:, :, P], 1e-5, None, ALU.add).then_inc(vec_back_step, 1)
                    dve.wait_ge(vec_back_step, back_step.next())
                    V.reciprocal(n, n).then_inc(vec_back_step, 1)
                    dve.wait_ge(vec_back_step, back_step.next())
                    for j in range(2):
                        a = slice(j * DH, (j + 1) * DH)
                        last = V.tensor_tensor(token[a, 2 * g:2 * g + 2, a], bank[a, :, a],
                                               n[a, :].unsqueeze(2).to_broadcast([DH, 2, DH]), ALU.mult)
                    last.then_inc(rest.free_of(f"token{g}"), 1)

            def token_shift(B):
                dve.wait_ge(*rest.holds("s2", B))
                bank = rest.bank("s2")[:, 0:PAIRS * SLICES].rearrange("p (c k) -> p c k", c=PAIRS)
                V.tensor_reduce(amax[:, :], bank, AX, ALU.max).then_inc(vec_back_step, 1)
                dve.wait_ge(vec_back_step, back_step.next())
                V.tensor_tensor(ash[:, :, :], bank, amax[:, :].unsqueeze(2).to_broadcast([P, PAIRS, SLICES]),
                                ALU.subtract).then_inc(rest.free_of("s2"), 1)

            def token_attn(B):
                dve.wait_ge(attn_exped, B.count(1, 1))
                V.tensor_reduce(asum[:, :], aexp[:, :, :], AX, ALU.add).then_inc(vec_back_step, 1)
                dve.wait_ge(vec_back_step, back_step.next())
                V.reciprocal(asum[:, :], asum[:, :]).then_inc(vec_back_step, 1)
                dve.wait_ge(vec_back_step, back_step.next())
                for j in range(2):
                    a = slice(j * DH, (j + 1) * DH)
                    last = V.tensor_tensor(attn[a, :, a], aexp[a, :, :],
                                           asum[a, :].unsqueeze(2).to_broadcast([DH, PAIRS, SLICES]), ALU.mult)
                last.then_inc(attn_ready, 1)

            def outputs(B, ts):
                if ts[0] == 0:
                    dve.wait_ge(h2_biased, B.count(1, 1))
                    if B.back(1).exists():
                        dve.wait_ge(out_stored, B.back(1).count(32, 32))
                for t in ts:
                    dve.wait_ge(*rest.holds(f"out{t}", B))
                    V.tensor_tensor(res[0:ROWS, t, :], rest.bank(f"out{t}")[0:ROWS, 0:E], h2[0:ROWS, t, :],
                                    ALU.add).then_inc(rest.free_of(f"out{t}"), 1)

            def body(B, F, G):
                if B is not None:
                    row_maxima(B, HEAD[0])
                if F is not None:
                    gram(F, [0])
                if B is not None:
                    row_maxima(B, HEAD[1])
                if F is not None:
                    gram(F, [1])
                if B is not None:
                    row_maxima(B, HEAD[2])
                    maxima_parts(B)
                if F is not None:
                    gram(F, [2, 3])
                    neighbours(F, T4[0:2])
                    neighbours(F, T4[2:])
                if B is not None:
                    norm(B, 0)
                    norm(B, 1)
                if F is not None:
                    low_qk(F, "q", [0])
                if B is not None:
                    norm(B, 2)
                if F is not None:
                    low_qk(F, "q", [1])
                if B is not None:
                    norm(B, 3)
                if F is not None:
                    low_qk(F, "q", [2, 3])
                if B is not None:
                    proj(B)
                if F is not None:
                    low_qk(F, "k", [0, 1])
                if B is not None:
                    normed(B, h2, mv2, z2, rstd2, rstd2_ready, z2_ready)
                if F is not None:
                    low_qk(F, "k", [2, 3])
                if B is not None:
                    low_transposed(rest, "z2T", z2T_high, z2T_l, z2T_h, B)
                if F is not None:
                    low_vals(F, [0, 1])
                if B is not None:
                    ffn_shift(B)
                    ffn_softmax(B)
                if F is not None:
                    low_vals(F, [2, 3])
                if B is not None:
                    tokens(B)
                for n in range(6):
                    if F is not None:
                        row_maxima(F, TAIL[n][0:1])
                    if B is not None and n == 3:
                        token_attn(B)
                    if F is not None:
                        row_maxima(F, TAIL[n][1:])
                    if G is not None:
                        tok(G, TOK_WHOLE[n])
                    if B is not None and n == 2:
                        token_shift(B)
                if G is not None:
                    tok_norm(G)
                if B is not None:
                    outputs(B, T4[0:3])
                if F is not None:
                    row_maxima(F, LATE)
                if G is not None:
                    low_transposed(front, "zT", zT_high, zT_l, zT_h, G)
                if B is not None:
                    outputs(B, T4[3:])

            over_images(dve, body)

        @block.gpsimd
        def _(pool):
            G = nc.gpsimd
            root1_step = Steps(1)
            root2_step = Steps(1)
            pool.wait_ge(setup_vec, 1)
            pool.wait_ge(consts_in, 16 * len(consts))

            def low_probs(B, hd):
                for t in T4:
                    pool.wait_ge(probs_split, B.count(HEADS * NT, hd * NT + t + 1))
                    pool.wait_ge(*scores.gone(f"sT{hd}_{t}", B))
                    G.tensor_tensor(probs_l[hd % 2][0:ROWS, t, :], probs[hd % 2][0:ROWS, t, :],
                                    probs_h[hd % 2][0:ROWS, t, :], ALU.subtract).then_inc(probs_ready, 1)

            def root(steps, step_sem, img, var_sem, mv, ve, rstd, rstd_sem):
                steps.begin(img)
                pool.wait_ge(var_sem, img.count(1, 1))
                G.tensor_tensor(ve[0:ROWS, :], mv[0:ROWS, :, 1], eps_s[0:ROWS, :], ALU.add).then_inc(step_sem, 1)
                pool.wait_ge(step_sem, steps.next())
                G.tensor_tensor(rstd[0:ROWS, :], ve[0:ROWS, :], half_s[0:ROWS, :], ALU.pow).then_inc(rstd_sem, 1)

            def biased(img, x, bias, z_sem, done):
                pool.wait_ge(z_sem, img.count(1, 1))
                G.tensor_tensor(x[0:ROWS, :, :], x[0:ROWS, :, :],
                                bias[0:ROWS, :].unsqueeze(1).to_broadcast([ROWS, NT, E]), ALU.add)\
                 .then_inc(done, 1)

            def body(B, F, G):
                if B is not None:
                    for hd in H8:
                        low_probs(B, hd)
                    root(root2_step, pool_root2_step, B, var2_ready, mv2, ve2, rstd2, rstd2_ready)
                    biased(B, h2, bout2_s, z2_ready, h2_biased)
                if G is not None:
                    root(root1_step, pool_root1_step, G, var1_ready, mv1, ve1, rstd1, rstd1_ready)
                    biased(G, h[par(G)], bout_s, z_ready, h_biased)

            over_images(pool, body)


def kernel(**inputs):
    import numpy as np
    import ml_dtypes
    import concourse.bacc as bacc
    from concourse.bass_utils import run_bass_kernel_spmd

    a = {k: np.asarray(w) for k, w in inputs.items()}

    def chunks(w):
        return w.reshape(-1, P, w.shape[1]).transpose(1, 0, 2)

    def rows(w):
        return np.broadcast_to(w.reshape(1, -1), (P, w.size))

    def twice(w):
        d = np.zeros((P, P), w.dtype)
        d[:DH, :DH] = w
        d[DH:, DH:] = w
        return d

    x = a["x"].reshape(BATCH, CHANNELS, GRID, PATCH, GRID, PATCH).transpose(0, 1, 3, 5, 2, 4)
    xt = np.zeros((BATCH, P, KT, NP), x.dtype)
    xt[..., :TOKENS] = x.reshape(BATCH, KT, P, TOKENS).transpose(0, 2, 1, 3)

    bf = ml_dtypes.bfloat16
    diag = np.zeros((P, NT, NP), np.float32)
    pick = np.zeros((P, HEADS, ROWS), np.float32)
    for t in range(NT):
        diag[np.arange(ROWS), t, t * ROWS + np.arange(ROWS)] = DIAG
        diag[:, t, TOKENS:] = DIAG
    for hd in range(HEADS):
        pick[hd, hd, :] = pick[HEADS + hd, hd, :] = 1
        pick[MAXROWS + np.arange(ROWS), hd, np.arange(ROWS)] = 1

    arrays = {
        "xt": xt,
        "wtok": chunks(a["L0_tok_W"].T),
        "btok": rows(a["L0_tok_b"]),
        "wqkv": chunks(a["L0_attn_Wqkv"]),
        "wout": chunks(a["L0_attn_Wout"]),
        "bout": rows(a["L0_attn_bout"]),
        "wfx": chunks(a["L0_ffn_W_fx"]),
        "bfx": rows(a["L0_ffn_b_fx"]),
        "wxT": chunks(a["L0_ffn_W_x"].T),
        "bx": a["L0_ffn_b_x"].reshape(PAIRS, P).T,
        "wslice": twice(a["L0_ffn_W_slice"]),
        "bslice": rows(np.tile(a["L0_ffn_b_slice"], HEADS)),
        "temp": rows(a["L0_ffn_temperature"]),
        "wqT2": twice(a["L0_ffn_W_q"].T),
        "wkT2": twice(a["L0_ffn_W_k"].T),
        "wvT2": twice(a["L0_ffn_W_v"].T),
        "wout2": chunks(a["L0_ffn_W_out"]),
        "bout2": rows(a["L0_ffn_b_out"]),
        "identf": np.eye(P, dtype=np.float32),
        "identb": np.eye(P, dtype=bf),
        "diag": diag.astype(bf),
        "pick": pick.astype(bf),
    }
    arrays = {k: np.ascontiguousarray(w) for k, w in arrays.items()}
    nc = bacc.Bacc("TRN2", target_bir_lowering=False, num_devices=1)
    args = {k: nc.dram_tensor(k, w.shape, mybir.dt.from_np(w.dtype), kind="ExternalInput").ap()
            for k, w in arrays.items()}
    out = nc.dram_tensor("out", (BATCH, TOKENS, E), mybir.dt.float32, kind="ExternalOutput").ap()
    build(nc, out=out, **args)
    r = run_bass_kernel_spmd(nc, [arrays], core_ids=[0])
    return r.results[0]["out"]
```
